# Optimizing a Trainium2 kernel written in Bass

```python
import numpy as np
import jax
import jax.numpy as jnp

def _softmax(x, axis=-1):
    return jax.nn.softmax(x, axis=axis)

def _gelu(x):
    return jax.nn.gelu(x, approximate=True)

def _silu(x):
    return jax.nn.silu(x)

def _sigmoid(x):
    return jax.nn.sigmoid(x)

def _layernorm(x, axis=-1, eps=1e-05):
    m = jnp.mean(x, axis=axis, keepdims=True)
    v = jnp.var(x, axis=axis, keepdims=True)
    return (x - m) / jnp.sqrt(v + eps)

def _scatter_add(tgt, idx, src, axis=0):
    return tgt.at[idx].add(src)

def _segment_sum(src, seg, n):
    return jax.ops.segment_sum(src, seg, n)
kernel_name = 'mk_xattn_ffn_d2_seqx_r4_64356c'

def setup_inputs(seed: int=0):
    np.random.seed(seed)
    _w = jnp.asarray

    def _rec_inputs():
        import jax
        import jax.numpy as jnp
        _rk = jax.random.key(seed)
        x = -0.0005207 + 1.001 * jax.random.normal(jax.random.fold_in(_rk, 1), (16, 128, 512), jnp.float32)
        _lenS = 128 - jax.random.randint(jax.random.fold_in(_rk, 7), (16,), 0, max(1, 128 // 4) + 1, jnp.int32)
        _lenS2 = 128 - jax.random.randint(jax.random.fold_in(_rk, 8), (16,), 0, max(1, 128 // 4) + 1, jnp.int32)
        _ctx_2048P = jax.random.normal(jax.random.fold_in(_rk, 12), (16, 16, 512), jnp.float32)
        _ctx_2048c = jax.random.dirichlet(jax.random.fold_in(_rk, 512), 0.3 * jnp.ones((16,), jnp.float32), (16, 128))
        _ctx_2048t = jnp.einsum('bsk,bkd->bsd', _ctx_2048c, _ctx_2048P)
        _ctx_2048t = _ctx_2048t * jax.lax.rsqrt(jnp.mean(jnp.square(_ctx_2048t)) + 1e-12) * 0.953939
        ctx_2048 = -5.72187e-05 + 0.999849 * (_ctx_2048t + 0.3 * jax.random.normal(jax.random.fold_in(_rk, 612), (16, 128, 512), jnp.float32))
        _validS = jnp.arange(128)[None, :] < _lenS[:, None]
        _validS2 = jnp.arange(128)[None, :] < _lenS2[:, None]
        _causal = jnp.tril(jnp.ones((128, 128), dtype=bool))
        mask_BxSx4224_bf0 = jnp.logical_not(jnp.ones((16, 128, 1056), dtype=bool))
        return (x, ctx_2048, mask_BxSx4224_bf0)
    x, ctx_2048, mask_BxSx4224_bf0 = _rec_inputs()

    def _L0_xattn_setup():
        import jax, jax.numpy as jnp
        import numpy as np
        import math
        DIM = 512
        B, Q_LEN, KV_LEN = (8, 128, 1024)
        key = jax.random.key(seed)
        ks = jax.random.split(key, 8)
        x = jax.random.normal(ks[0], (B, Q_LEN, DIM), dtype=jnp.float32)
        mask = jnp.zeros((B, Q_LEN, KV_LEN + Q_LEN), dtype=bool)
        k_cache = jax.random.normal(ks[1], (B, KV_LEN, DIM), dtype=jnp.float32)
        v_cache = jax.random.normal(ks[2], (B, KV_LEN, DIM), dtype=jnp.float32)
        scale = 1.0 / math.sqrt(DIM)
        wq = jax.random.normal(ks[3], (DIM, DIM), dtype=jnp.float32) * scale
        wk = jax.random.normal(ks[4], (DIM, DIM), dtype=jnp.float32) * scale
        wv = jax.random.normal(ks[5], (DIM, DIM), dtype=jnp.float32) * scale
        wo = jax.random.normal(ks[6], (DIM, DIM), dtype=jnp.float32) * scale
        return {'x': x, 'mask': mask, 'k_cache': k_cache, 'v_cache': v_cache, 'wq': wq, 'wk': wk, 'wv': wv, 'wo': wo}
    _L0_xattn_all = _L0_xattn_setup()
    _L0_xattn_in = {k: v for k, v in _L0_xattn_all.items() if k in ('wq', 'wk', 'wv', 'wo')}
    del _L0_xattn_all

    def _L0_ffn_setup():
        import jax, jax.numpy as jnp
        import numpy as np
        B, S, D = (4, 512, 512)
        E, F, K = (8, 256, 2)
        SF = 256
        EPS = 1e-06

        def _rmsnorm(x, w, eps=EPS):
            var = jnp.mean(x * x, axis=-1, keepdims=True)
            return x * jax.lax.rsqrt(var + eps) * w
        key = jax.random.key(seed)
        ks = jax.random.split(key, 9)
        g = lambda k, shape, scale: jax.random.normal(k, shape, jnp.float32) * scale
        return {'x': g(ks[0], (B, S, D), 1.0), 'rms_weight': jnp.ones((D,), jnp.float32), 'router_w': g(ks[1], (D, E), 0.02), 'w_gate': g(ks[2], (E, D, F), 0.02), 'w_up': g(ks[3], (E, D, F), 0.02), 'w_down': g(ks[4], (E, F, D), 0.02), 'sw_gate': g(ks[5], (D, SF), 0.02), 'sw_up': g(ks[6], (D, SF), 0.02), 'sw_down': g(ks[7], (SF, D), 0.02)}
    _L0_ffn_all = _L0_ffn_setup()
    _L0_ffn_in = {k: v for k, v in _L0_ffn_all.items() if k in ('rms_weight', 'router_w', 'w_gate', 'w_up', 'w_down', 'sw_gate', 'sw_up', 'sw_down')}
    del _L0_ffn_all

    def _L1_xattn_setup():
        import jax, jax.numpy as jnp
        import numpy as np
        N_HEAD = 8
        key = jax.random.key(seed)
        k1, k2, k3 = jax.random.split(key, 3)
        b, d, m = (4, 256, 512)
        c, n = (256, 512)
        q = jax.random.normal(k1, (b, d, m), dtype=jnp.float32)
        k = jax.random.normal(k2, (d // d * b, d, n), dtype=jnp.float32).reshape(b, d, n)
        v = jax.random.normal(k3, (b, c, n), dtype=jnp.float32)
        return {'q': q, 'k': k, 'v': v}
    _L1_xattn_all = _L1_xattn_setup()
    _L1_xattn_in = {k: v for k, v in _L1_xattn_all.items() if k in ()}
    del _L1_xattn_all

    def _L1_ffn_setup():
        import jax, jax.numpy as jnp
        import numpy as np
        TOP_K = 2
        NUM_EXPERTS = 8
        ROUTE_SCALE = 1.0
        key = jax.random.key(seed)
        ks = jax.random.split(key, 8)
        bs, slen, dim, hidden, E = (4, 256, 512, 256, NUM_EXPERTS)
        s = 0.02
        return {'x': jax.random.normal(ks[0], (bs, slen, dim), jnp.float32), 'gate_w': jax.random.normal(ks[1], (E, dim), jnp.float32) * s, 'w1': jax.random.normal(ks[2], (E, hidden, dim), jnp.float32) * s, 'w2': jax.random.normal(ks[3], (E, dim, hidden), jnp.float32) * s, 'w3': jax.random.normal(ks[4], (E, hidden, dim), jnp.float32) * s, 'ws1': jax.random.normal(ks[5], (hidden, dim), jnp.float32) * s, 'ws2': jax.random.normal(ks[6], (dim, hidden), jnp.float32) * s, 'ws3': jax.random.normal(ks[7], (hidden, dim), jnp.float32) * s}
    _L1_ffn_all = _L1_ffn_setup()
    _L1_ffn_in = {k: v for k, v in _L1_ffn_all.items() if k in ('gate_w', 'w1', 'w2', 'w3', 'ws1', 'ws2', 'ws3')}
    del _L1_ffn_all
    return {'x': x, 'ctx_2048': ctx_2048, 'mask_BxSx4224_bf0': mask_BxSx4224_bf0, 'L0_xattn_wq': _L0_xattn_in['wq'], 'L0_xattn_wk': _L0_xattn_in['wk'], 'L0_xattn_wv': _L0_xattn_in['wv'], 'L0_xattn_wo': _L0_xattn_in['wo'], 'L0_ffn_rms_weight': _L0_ffn_in['rms_weight'], 'L0_ffn_router_w': _L0_ffn_in['router_w'], 'L0_ffn_w_gate': _L0_ffn_in['w_gate'], 'L0_ffn_w_up': _L0_ffn_in['w_up'], 'L0_ffn_w_down': _L0_ffn_in['w_down'], 'L0_ffn_sw_gate': _L0_ffn_in['sw_gate'], 'L0_ffn_sw_up': _L0_ffn_in['sw_up'], 'L0_ffn_sw_down': _L0_ffn_in['sw_down'], 'L1_ffn_gate_w': _L1_ffn_in['gate_w'], 'L1_ffn_w1': _L1_ffn_in['w1'], 'L1_ffn_w2': _L1_ffn_in['w2'], 'L1_ffn_w3': _L1_ffn_in['w3'], 'L1_ffn_ws1': _L1_ffn_in['ws1'], 'L1_ffn_ws2': _L1_ffn_in['ws2'], 'L1_ffn_ws3': _L1_ffn_in['ws3']}

def reference(x, ctx_2048, mask_BxSx4224_bf0, L0_xattn_wq, L0_xattn_wk, L0_xattn_wv, L0_xattn_wo, L0_ffn_rms_weight, L0_ffn_router_w, L0_ffn_w_gate, L0_ffn_w_up, L0_ffn_w_down, L0_ffn_sw_gate, L0_ffn_sw_up, L0_ffn_sw_down, L1_ffn_gate_w, L1_ffn_w1, L1_ffn_w2, L1_ffn_w3, L1_ffn_ws1, L1_ffn_ws2, L1_ffn_ws3):
    import jax
    import jax.numpy as jnp

    def _L0_xattn_ref(x, mask, k_cache, v_cache, wq, wk, wv, wo):
        import jax, jax.numpy as jnp
        import numpy as np
        import math
        DIM = 512
        B, Q_LEN, KV_LEN = (8, 128, 1024)
        q = jnp.einsum('bsd,ed->bse', x, wq)
        k_new = jnp.einsum('bsd,ed->bse', x, wk)
        v_new = jnp.einsum('bsd,ed->bse', x, wv)
        k = jnp.concatenate([k_cache, k_new], axis=1)
        v = jnp.concatenate([v_cache, v_new], axis=1)
        scale = 1.0 / math.sqrt(q.shape[-1])
        scores = jnp.einsum('bqd,bkd->bqk', q, k) * scale
        attn = jax.nn.softmax(scores, axis=-1)
        out = jnp.einsum('bqk,bkd->bqd', attn, v)
        return jnp.einsum('bqd,ed->bqe', out, wo)

    def _L0_ffn_ref(x, rms_weight, router_w, w_gate, w_up, w_down, sw_gate, sw_up, sw_down):
        import jax, jax.numpy as jnp
        import numpy as np
        B, S, D = (4, 512, 512)
        E, F, K = (8, 256, 2)
        SF = 256
        EPS = 1e-06

        def _rmsnorm(x, w, eps=EPS):
            var = jnp.mean(x * x, axis=-1, keepdims=True)
            return x * jax.lax.rsqrt(var + eps) * w
        b, s, d = x.shape
        e = router_w.shape[1]
        h = _rmsnorm(x, rms_weight)
        ht = h.reshape(-1, d)
        t = ht.shape[0]
        logits = ht @ router_w
        probs = jax.nn.softmax(logits, axis=-1)
        topv, topi = jax.lax.top_k(probs, K)
        topv = topv / jnp.sum(topv, axis=-1, keepdims=True)
        w_dense = jnp.zeros((t, e), ht.dtype).at[jnp.arange(t)[:, None], topi].set(topv)
        g = jnp.einsum('td,edf->tef', ht, w_gate)
        u = jnp.einsum('td,edf->tef', ht, w_up)
        eo = jnp.einsum('tef,efd->ted', jax.nn.silu(g) * u, w_down)
        moe = jnp.einsum('te,ted->td', w_dense, eo)
        sh = jax.nn.silu(ht @ sw_gate) * (ht @ sw_up) @ sw_down
        return (moe + sh).reshape(b, s, d)

    def _L1_xattn_ref(q, k, v):
        import jax, jax.numpy as jnp
        import numpy as np
        N_HEAD = 8
        b, d, m = q.shape
        c = v.shape[1]
        h = N_HEAD
        qh = q.reshape(b * h, d // h, m)
        kh = k.reshape(b * h, d // h, -1)
        vh = v.reshape(b * h, c // h, -1)
        scale = 1.0 / jnp.sqrt(jnp.asarray(d // h, dtype=q.dtype))
        qk = jnp.einsum('bdm,bdn->bmn', qh, kh) * scale
        sm = jax.nn.softmax(qk, axis=-1)
        ret = jnp.einsum('bmn,bcn->bcm', sm, vh)
        return ret.reshape(b, c, m)

    def _L1_ffn_ref(x, gate_w, w1, w2, w3, ws1, ws2, ws3):
        import jax, jax.numpy as jnp
        import numpy as np
        TOP_K = 2
        NUM_EXPERTS = 8
        ROUTE_SCALE = 1.0
        bs, slen, dim = x.shape
        xf = x.reshape(-1, dim)
        logits = (xf @ gate_w.T).astype(jnp.float32)
        scores = jax.nn.sigmoid(logits)
        top_scores, sel_idx = jax.lax.top_k(scores, TOP_K)
        top_scores = top_scores * ROUTE_SCALE
        routed = jnp.zeros_like(xf)
        for k in range(TOP_K):
            xs = xf * top_scores[:, k][:, None]
            h1 = jnp.einsum('td,ehd->teh', xs, w1)
            h3 = jnp.einsum('td,ehd->teh', xs, w3)
            h = jax.nn.silu(h1) * h3
            onehot = jax.nn.one_hot(sel_idx[:, k], NUM_EXPERTS, dtype=h.dtype)
            routed = routed + jnp.einsum('teh,te,edh->td', h, onehot, w2)
        shared = jax.nn.silu(xf @ ws1.T) * (xf @ ws3.T) @ ws2.T
        out = (shared + routed).reshape(bs, slen, dim)
        return out
    x = x + _L0_xattn_ref(_layernorm(x, axis=-1), mask_BxSx4224_bf0, ctx_2048, ctx_2048, L0_xattn_wq, L0_xattn_wk, L0_xattn_wv, L0_xattn_wo)
    x = x + _L0_ffn_ref(_layernorm(x, axis=-1), L0_ffn_rms_weight, L0_ffn_router_w, L0_ffn_w_gate, L0_ffn_w_up, L0_ffn_w_down, L0_ffn_sw_gate, L0_ffn_sw_up, L0_ffn_sw_down)
    x = x + _L1_xattn_ref(_layernorm(x, axis=-1), ctx_2048, ctx_2048)
    x = x + _L1_ffn_ref(_layernorm(x, axis=-1), L1_ffn_gate_w, L1_ffn_w1, L1_ffn_w2, L1_ffn_w3, L1_ffn_ws1, L1_ffn_ws2, L1_ffn_ws3)
    return x

_drawn_inputs = setup_inputs


def setup_inputs(seed=0):
    import zlib

    import numpy as np

    out = dict(_drawn_inputs(seed))
    spreads = {'L0_ffn_rms_weight': (1.0, 0.6)}
    factors = {'L1_ffn_gate_w': 4.719,
     'L1_ffn_w1': 4.148,
     'L1_ffn_w2': 4.098,
     'L1_ffn_w3': 4.104,
     'L1_ffn_ws1': 5.967,
     'L1_ffn_ws2': 5.849,
     'L1_ffn_ws3': 5.911}
    for name, (base, spread) in spreads.items():
        noise = np.random.default_rng([zlib.crc32(name.encode()), seed]).standard_normal(out[name].shape)
        drawn = base * np.exp(spread * noise) if base else spread * noise
        out[name] = jnp.asarray(drawn.astype(out[name].dtype))
    for name, factor in factors.items():
        out[name] = (out[name] * factor).astype(out[name].dtype)
    return out
```

```python
from contextlib import ExitStack

import numpy as np
import concourse.bass as bass
from concourse import mybir

F32 = mybir.dt.float32
F16 = mybir.dt.float16
BF16 = mybir.dt.bfloat16
I32 = mybir.dt.int32
ALU = mybir.AluOpType
ACT = mybir.ActivationFunctionType
AX = mybir.AxisListType

P = 128
D = 512
DT = D // P
B = 16
T = B * P
NT = T // P
G = 4
NG = NT // G
E = 8
NE = E + 1
F = 256
FT = F // P
JOBS = 2 * T // P + E - 1
H = 8
HD = P // H
SLOTS = 6
KR = SLOTS * HD
MAX_PARTS = 2
KM = KR + MAX_PARTS
K_PARTS = (0, 1, 2, 0, 1, 0)
Q_PARTS = (0, 0, 0, 1, 1, 2)
QUADS = NT * 2
CHUNKS = NE * DT
CPG = CHUNKS // NG

XS = 1024.0
WS = 256.0
UNSCALE = 1.0 / (XS * WS)
SCORE = float(D) ** -0.5
HEAD_SCORE = float(HD) ** -0.5
HI, LO = 0, 1


def build(nc, a, out):
    ctx = ExitStack()
    with ctx:
        def sem(name):
            return ctx.enter_context(nc.semaphore(name))

        def sb(name, shape, dt):
            return ctx.enter_context(nc.sbuf_tensor("sb_" + name, shape, dt))

        x = sb("x", [P, NT, D], F32)
        wgu = sb("wgu", [P, CHUNKS, 2, 2 * F], F16)
        ident = sb("ident", [P, P], F32)
        ident16 = sb("ident16", [P, P], F16)
        stats = sb("stats", [P, 2, 6], F32)
        mvt = sb("mvt", [P, 2, 2], F32)
        mv = sb("mv", [P, NT, 2], F32)
        rstd = sb("rstd", [P, NT], F32)
        shift = sb("shift", [P, NT], F32)
        lnt = sb("lnt", [P, NT], F32)
        mhalf = sb("mhalf", [P, NT], F32)
        wsc = sb("wsc", [P, 2, CHUNKS], F32)
        rw = sb("rw", [P, DT, E], F32)
        rwp = sb("rwp", [P, DT, 2, E], F16)
        ps = ctx.enter_context(nc.psum_tensor("ps", [P, 8, 512], F32))

        WORDS = 25870
        pool_mem = sb("shared", [P, WORDS], F32)

        class Carve:
            def __init__(self):
                self.at = 0

            def __call__(self, shape, dt):
                n = int(np.prod(shape))
                words = n if dt in (F32, I32) else (n + 1) // 2
                v = pool_mem[:, self.at:self.at + words]
                self.at += words
                assert self.at <= WORDS, self.at
                if dt != F32:
                    v = v.bitcast(dt)
                names = " ".join("abcd"[:len(shape)])
                sizes = {"abcd"[i]: s for i, s in enumerate(shape)}
                return v.rearrange(f"p ({names}) -> p {names}", **sizes) if len(shape) > 1 else v

        kst = nc.dram_tensor("kst", [B, KR, H, D], BF16).ap()
        qst = nc.dram_tensor("qst", [2, KR, H, D], BF16).ap()
        hrow = nc.dram_tensor("hrow", [T, 2 * D], F16).ap()
        xslot = nc.dram_tensor("xslot", [JOBS * P, D + 1], I32).ap()
        yslot = nc.dram_tensor("yslot", [JOBS * P, D], F32).ap()

        x_tiles = a["x"]
        gu_chunks = [a["L0_gu"], a["L1_gu"]]

        c1 = Carve()
        w3 = c1([3, 2, DT, D], F16)
        wo = c1([DT, D], F32)
        rows1 = c1([G, 2, D], F16)
        xt1_words = c1.at
        xt1 = c1([2, DT, G, P], F16)
        xn1 = c1([D], F32)
        qt_at = c1.at
        qt = c1([DT, G, P], F32)
        kt_at = c1.at
        kt = c1([DT, G, P], F32)
        v1 = c1([G, D], F32)
        ct1 = c1([G, DT, P], F32)
        cx1 = c1([G, D], F32)
        kparts = c1([3, D], BF16)
        krest = c1([D], F32)
        stage = c1([3, D], F32)
        zeros = wgu[:, 20:22, :, :].rearrange("p c h f -> p (c h f)")[:, 0:2 * D + 2]
        small1 = c1([3, G], F32)
        negmax1, rowsum1, rinv1 = small1[:, 0, :], small1[:, 1, :], small1[:, 2, :]
        prob1 = pool_mem[:, xt1_words:xt1_words + G * 256].rearrange("p (g k) -> p g k", g=G)
        probt1 = pool_mem[:, kt_at:kt_at + G * 256].rearrange("p (g k q) -> p g k q", g=G, k=2)
        ot1 = pool_mem[:, qt_at:qt_at + G * D].rearrange("p (g e q) -> p g e q", g=G, e=DT)
        wstage = [wgu[:, CHUNKS - 4 * (j + 1):CHUNKS - 4 * j, :, :].rearrange("p c h f -> p (c h f)")
                  .bitcast(F32).rearrange("p (t n) -> p t n", t=DT) for j in range(3)]

        c2 = Carve()
        wd = c2([NE, FT, D], F32)
        rowout = c2([2, 2, D], F16)
        xn2 = c2([2, D], F32)
        xt2 = c2([2, 2, DT, P], F16)
        rowa = c2([4, 2 * D + 2], F16)
        rowb = c2([4, 2 * D + 2], F16)
        rowin = c2([4, 2 * D + 2], F16)
        sg = c2([2, F], F32)
        hid = c2([2, F], F32)
        ht = c2([2, FT, P], F32)
        yb = c2([2, D], F32)
        gy = c2([2, 2, D], F32)
        lg, m1, m2, asg, cum, z, em8, scanmask = [c2([E, NT], F32) for _ in range(8)]
        top1, top2, idx1, idx2, w1, w2, ex = [c2([NT], F32) for _ in range(7)]
        pos1, pos2 = c2([NT], I32), c2([NT], I32)
        s12 = c2([2, NT], F32)
        tiles_i = c2([E], I32)
        tiles_f, tiles_c, base, ones8, startpos = [c2([E], F32) for _ in range(5)]
        jidx, jexp = c2([JOBS], F32), c2([JOBS], F32)
        eid = c2([JOBS], I32)
        tri = c2([P], F32)
        ones = c2([P], F32)
        icol = c2([4, 2], I32)
        unscale = c2([1], F32)

        c3 = Carve()
        ks = c3([4, 4, D], BF16)
        qs = c3([4, 4, D], BF16)
        prob3 = c3([2, 4, D], F32)
        va = c3([2, DT, H, 2 * HD], F32)
        ct3 = c3([2, DT, P], F32)
        qn = c3([D], F32)
        qparts = c3([3, D], BF16)
        osb = c3([2, D], F32)
        num = c3([2, D], F32)
        den = c3([2, D], F32)
        stage3 = c3([3, D], F32)
        mx = c3([2, 16], F32)
        nm = c3([MAX_PARTS, P], BF16)

        consts, mhalf_set, zero_set, zero_out = sem("consts"), sem("mhalf_set"), sem("zero_set"), sem("zero_out")
        x_in = [sem(f"x_in{g}") for g in range(NG)]
        w_in = [sem(f"w_in{j}") for j in range(3)]
        wo_in, rms_in, scales = sem("wo_in"), sem("rms_in"), sem("scales")
        w_hi, w_lo = sem("w_hi"), sem("w_lo")
        stat_step, stats_rdy = sem("stat_step"), [sem(f"stats_rdy{k}") for k in range(4)]
        factors = [sem(f"factors{k}") for k in range(4)]
        rw_in, rw_step = [sem(f"rw_in{k}") for k in range(2)], [sem(f"rw_step{k}") for k in range(2)]

        xn_rdy, hi_rdy, row_rdy = sem("xn_rdy"), sem("hi_rdy"), sem("row_rdy")
        t_ps, xt_rdy = sem("t_ps"), sem("xt_rdy")
        q_ps, q_rdy = sem("q_ps"), sem("q_rdy")
        k_ps, k_rdy = sem("k_ps"), sem("k_rdy")
        v_ps, v_rdy = sem("v_ps"), sem("v_rdy")
        s_ps, max_rdy, prob_rdy = sem("s_ps"), sem("max_rdy"), sem("prob_rdy")
        pt_ps, pt_rdy = sem("pt_ps"), sem("pt_rdy")
        o_ps, o_rdy = sem("o_ps"), sem("o_rdy")
        y_ps, rinv_rdy, x1_done = sem("y_ps"), sem("rinv_rdy"), sem("x1_done")
        ct_in, cx_in = sem("ct_in"), sem("cx_in")
        kp_step, kp_rdy, kp_out = sem("kp_step"), sem("kp_rdy"), sem("kp_out")
        chunk_in = [[sem(f"chunk_in{k}_{u}") for u in range(3)] for k in range(2)]
        chunk_step = sem("chunk_step")

        held = sem("held")

        def wait_apart(eng, what, value):
            eng.wait_ge(what, value)
            if not isinstance(value, int):
                eng.nop().then_inc(held, 1)

        def later(n, least):
            return not isinstance(n, int) or n >= least

        def earlier(n, bound):
            return not isinstance(n, int) or n < bound

        def steps(eng, total, head, tail, unroll, step):
            assert head % unroll == 0 and (total - head - tail) % unroll == 0
            for n in range(head):
                step(n, n % unroll, n // unroll)
            with eng.Fori(0, (total - head - tail) // unroll) as i:
                for u in range(unroll):
                    step(i * unroll + (head + u), u, i + head // unroll)
            for n in range(total - tail, total):
                step(n, n % unroll, n // unroll)

        def tile_stats(dve, n, done, u, k, after=None, count=None):
            if after is not None:
                wait_apart(dve, after, count)
            dve.bn_stats(stats[:, u, :], x[:, n, :]).then_inc(stat_step, 1)
            wait_apart(dve, stat_step, done * 2 + 1)
            dve.bn_aggr(mvt[:, u, :], stats[:, u, :]).then_inc(stat_step, 1)
            wait_apart(dve, stat_step, done * 2 + 2)
            dve.tensor_copy(mv[:, n, :], mvt[:, u, :]).then_inc(stats_rdy[k], 1)

        FACTOR_STEPS = {False: 5, True: 10}

        def norm_factors(k, scale, rms):
            pool = nc.gpsimd
            pool.wait_ge(stats_rdy[k], NT)
            n = 0

            def then(ins):
                nonlocal n
                n += 1
                ins.then_inc(factors[k], 1)
                pool.wait_ge(factors[k], n)

            var, mean = mv[:, :, 1], mv[:, :, 0]
            then(pool.tensor_scalar(lnt[:], var, 1.0, 1e-5, ALU.mult, ALU.add))
            then(pool.tensor_tensor(rstd[:], lnt[:], mhalf[:], ALU.pow))
            if rms:
                then(pool.tensor_tensor(lnt[:], rstd[:], rstd[:], ALU.mult))
                then(pool.tensor_tensor(lnt[:], lnt[:], var, ALU.mult))
                then(pool.tensor_scalar(lnt[:], lnt[:], 1.0, 1e-6, ALU.mult, ALU.add))
                then(pool.tensor_tensor(lnt[:], lnt[:], mhalf[:], ALU.pow))
                then(pool.tensor_tensor(rstd[:], rstd[:], lnt[:], ALU.mult))
            then(pool.tensor_scalar(rstd[:], rstd[:], scale, 1.0, ALU.mult, ALU.mult))
            then(pool.tensor_tensor(lnt[:], mean, rstd[:], ALU.mult))
            then(pool.tensor_scalar(shift[:], lnt[:], -1.0, 1.0, ALU.mult, ALU.mult))
            assert n == FACTOR_STEPS[rms]

        def prepare_chunk(k, buf, c, j, r, u):
            pool = nc.gpsimd
            wait_apart(pool, chunk_in[k][u], 16 * (r + 1))
            scale = wsc[:, k, bass.ds(c, 1)].broadcast_to([P, 2 * F])
            pool.tensor_tensor(wgu[:, c, HI, :], buf, scale, ALU.mult).then_inc(chunk_step, 1)
            wait_apart(pool, chunk_step, k * 3 * CHUNKS + c * 3 + 1)
            pool.tensor_tensor(buf, buf, scale, ALU.mult).then_inc(chunk_step, 1)
            wait_apart(pool, chunk_step, k * 3 * CHUNKS + c * 3 + 2)
            pool.tensor_tensor(wgu[:, c, LO, :], buf, wgu[:, c, HI, :], ALU.subtract).then_inc(chunk_step, 1)

        def load_chunk(sp, k, buf, c, u, r):
            if k == 1 or later(c, 3):
                sp.wait_ge(chunk_step, c * 3 + (k * 3 * CHUNKS - 6))
            sp.dma_start(buf, a[f"L{k}_gu"][c]).then_inc(chunk_in[k][u], 16)

        def prepare_router(k):
            pool = nc.gpsimd
            pool.wait_ge(rw_in[k], 16)
            for t in range(DT):
                pool.tensor_scalar(rw[:, t, :], rw[:, t, :], wsc[:, k, t:t + 1], 1.0, ALU.mult, ALU.mult).then_inc(rw_step[k], 1)
            pool.wait_ge(rw_step[k], DT)
            pool.tensor_scalar(rwp[:, :, HI, :], rw[:], 1.0, 1.0, ALU.mult, ALU.mult).then_inc(rw_step[k], 1)
            pool.wait_ge(rw_step[k], DT + 1)
            pool.tensor_tensor(rwp[:, :, LO, :], rw[:], rwp[:, :, HI, :], ALU.subtract).then_inc(rw_step[k], 1)

        def attn1_sync(sp):
            xg = a["x"].rearrange("(g t p) d -> g p t d", t=G, p=P)
            for g in range(NG):
                if g < 3:
                    sp.dma_start(wstage[g], a[("wqT", "wkT", "wvT")[g]].rearrange("(t p) n -> p t n", p=P)).then_inc(w_in[g], 16)
                sp.dma_start(x[:, g * G:(g + 1) * G, :], xg[g]).then_inc(x_in[g], 16)
            sp.dma_start(wsc[:, 0, :], a["rms"]).then_inc(rms_in, 16)
            sp.dma_start(rw[:], a["L0_rw"]).then_inc(rw_in[0], 16)
            sp.dma_start(wo, a["woT"].rearrange("(t p) n -> p t n", p=P)).then_inc(wo_in, 16)
            ctT = a["ctxT"].rearrange("b (e p) s -> b p e s", p=P)
            cx = a["ctx"].rearrange("(g t p) d -> g p t d", t=G, p=P)

            def context(g):
                for t in range(G):
                    sp.dma_start(ct1[:, t, :, :], ctT[g * G + t]).then_inc(ct_in, 16)
                sp.dma_start(cx1, cx[g]).then_inc(cx_in, 16)

            context(0)
            sp.wait_ge(zero_set, 1)
            xz = xslot.rearrange("(j p) n -> j p n", p=P)
            with sp.Fori(0, JOBS) as j:
                sp.dma_start(xz[j], zeros.bitcast(I32)).then_inc(zero_out, 16)

            def group(g):
                for t in range(G):
                    sp.wait_ge(kp_rdy, g * G + (t + 1))
                    for s, part in enumerate(K_PARTS):
                        sp.dma_start(kst[g * G + t, s * HD:(s + 1) * HD].rearrange("d h m -> h d m"),
                                     kparts[:, part, :]).then_inc(kp_out, 16)
                for j in range(CPG):
                    load_chunk(sp, 0, stage[:, j % 3, :], g * CPG + j, j % 3, g * 3 + j // 3)
                if earlier(g, NG - 1):
                    sp.wait_ge(o_ps, g * G + G)
                    context(g + 1)

            steps(sp, NG, 1, 1, 1, lambda n, u, r: group(n))

        def attn1_gpsimd(pool):
            pool.memset(ident[:], 0.0).then_inc(consts, 1)
            pool.memset(ident16[:], 0.0).then_inc(consts, 1)
            pool.wait_ge(consts, 2)
            for m in (ident, ident16):
                pool.affine_select(out=m[:], in_=m[:], compare_op=ALU.not_equal, fill=1.0, base=0,
                                   pattern=[[-1, P]], channel_multiplier=1).then_inc(consts, 1)
            pool.memset(zeros, 0.0).then_inc(zero_set, 1)
            pool.memset(wsc[:, 1, :], WS).then_inc(scales, 1)
            pool.memset(mhalf[:], -0.5).then_inc(mhalf_set, 1)
            pool.wait_ge(mhalf_set, 1)
            norm_factors(0, XS, False)
            pool.wait_ge(rms_in, 16)
            pool.tensor_scalar(wsc[:, 0, :], wsc[:, 0, :], WS, 1.0, ALU.mult, ALU.mult).then_inc(scales, 1)
            pool.wait_ge(scales, 2)
            prepare_router(0)
            pool.wait_ge(w_lo, 3)

            def group(g):
                if later(g, 1):
                    pool.wait_ge(zero_out, 16 * JOBS)
                for t in range(G):
                    pool.wait_ge(cx_in, g * 16 + 16)
                    if later(g * G + t if isinstance(g, int) else g, 1):
                        wait_apart(pool, kp_out, (g * G + t) * (16 * SLOTS))
                    n = (g * G + t) * 4
                    pool.tensor_scalar(kparts[:, 0, :], cx1[:, t, :], 1.0, 1.0, ALU.mult, ALU.mult).then_inc(kp_step, 1)
                    wait_apart(pool, kp_step, n + 1)
                    pool.tensor_tensor(krest, cx1[:, t, :], kparts[:, 0, :], ALU.subtract).then_inc(kp_step, 1)
                    wait_apart(pool, kp_step, n + 2)
                    pool.tensor_scalar(kparts[:, 1, :], krest, 1.0, 1.0, ALU.mult, ALU.mult).then_inc(kp_step, 1)
                    wait_apart(pool, kp_step, n + 3)
                    pool.tensor_tensor(kparts[:, 2, :], krest, kparts[:, 1, :], ALU.subtract).then_inc(kp_step, 1)
                    pool.wait_ge(kp_step, n + 4)
                    pool.nop().then_inc(kp_rdy, 1)
                for j in range(CPG):
                    prepare_chunk(0, stage[:, j % 3, :], g * CPG + j, j, g * 3 + j // 3, j % 3)

            steps(pool, NG, 1, 1, 1, lambda n, u, r: group(n))

        def attn1_scalar(act):
            for j in range(3):
                act.wait_ge(w_in[j], 16)
                act.activation(w3[:, j, HI, :, :], wstage[j], ACT.Copy, scale=WS).then_inc(w_hi, 1)
            act.wait_ge(factors[0], FACTOR_STEPS[False])

            def normed(g):
                for t in range(G):
                    if later(g * G + t if isinstance(g, int) else g, 1):
                        act.wait_ge(row_rdy, g * G + t)
                    n = g * G + t
                    act.activation(xn1, x[:, n, :], ACT.Identity, scale=rstd[:, bass.ds(n, 1)],
                                   bias=shift[:, bass.ds(n, 1)]).then_inc(xn_rdy, 1)

            def group(g):
                for t in range(G):
                    act.wait_ge(t_ps, g * G + (t + 1))
                    act.activation(xt1[:, :, :, t, :], ps[:, t, :].bitcast(F16).rearrange("p (h e s) -> p h e s", h=2, e=DT),
                                   ACT.Copy).then_inc(xt_rdy, 1)
                for t in range(G):
                    act.wait_ge(q_ps, g * G + (t + 1))
                    act.activation(qt[:, t, :, :], ps[:, 4 + t, :].rearrange("p (t s) -> p t s", t=G), ACT.Copy,
                                   scale=UNSCALE * SCORE).then_inc(q_rdy, 1)
                if earlier(g, NG - 1):
                    normed(g + 1)
                for t in range(G):
                    act.wait_ge(max_rdy, g * G + (t + 1))
                    act.activation(prob1[:, t, :], ps[:, t, 0:2 * P], ACT.Exp, bias=negmax1[:, t:t + 1],
                                   accum_out=rowsum1[:, t:t + 1]).then_inc(prob_rdy, 1)
                for t in range(G):
                    act.wait_ge(pt_ps, g * G + (t + 1))
                    act.activation(probt1[:, t, :, :], ps[:, 4 + t, 0:2 * P].rearrange("p (k q) -> p k q", k=2),
                                   ACT.Copy).then_inc(pt_rdy, 1)

            normed(0)
            steps(act, NG, 1, 1, 1, lambda n, u, r: group(n))

        def attn1_vector(dve):
            for n in range(NT):
                if n % G == 0:
                    dve.wait_ge(x_in[n // G], 16)
                tile_stats(dve, n, n, n % 2, 0)
                if n % G == G - 1 and n // G < 3:
                    j = n // G
                    dve.wait_ge(w_hi, j + 1)
                    dve.scalar_tensor_tensor(out=w3[:, j, LO, :, :], in0=wstage[j], scalar=WS, in1=w3[:, j, HI, :, :],
                                             op0=ALU.mult, op1=ALU.subtract).then_inc(w_lo, 1)

            def rows(g):
                for t in range(G):
                    dve.wait_ge(xn_rdy, g * G + (t + 1))
                    dve.tensor_copy(rows1[:, t, HI, :], xn1).then_inc(hi_rdy, 1)
                    dve.wait_ge(hi_rdy, g * G + (t + 1))
                    dve.tensor_tensor(rows1[:, t, LO, :], xn1, rows1[:, t, HI, :],
                                      ALU.subtract).then_inc(row_rdy, 1)

            def group(g):
                for t in range(G):
                    dve.wait_ge(k_ps, g * G + (t + 1))
                    dve.tensor_scalar(kt[:, t, :, :], ps[:, t, :].rearrange("p (t s) -> p t s", t=G), UNSCALE, None,
                                      ALU.mult).then_inc(k_rdy, 1)
                for t in range(G):
                    dve.wait_ge(v_ps, g * G + (t + 1))
                    dve.tensor_scalar(v1[:, t, :], ps[:, 4 + t, :], UNSCALE, None, ALU.mult).then_inc(v_rdy, 1)
                for t in range(G):
                    dve.wait_ge(s_ps, g * G + (t + 1))
                    if later(g, 1):
                        dve.wait_ge(x1_done, (g - 1) * G + (t + 1))
                    dve.tensor_reduce(negmax1[:, t:t + 1], ps[:, t, 0:2 * P], AX.X, ALU.max,
                                      negate=True).then_inc(max_rdy, 1)
                if earlier(g, NG - 1):
                    rows(g + 1)
                for t in range(G):
                    dve.wait_ge(prob_rdy, g * G + (t + 1))
                    dve.reciprocal(rinv1[:, t:t + 1], rowsum1[:, t:t + 1]).then_inc(rinv_rdy, 1)
                for t in range(G):
                    dve.wait_ge(o_ps, g * G + (t + 1))
                    dve.tensor_copy(ot1[:, t, :, :], ps[:, t, :].rearrange("p (e q) -> p e q", e=DT)).then_inc(o_rdy, 1)
                dve.wait_ge(rinv_rdy, g * G + G)
                for t in range(G):
                    n = g * G + t
                    dve.wait_ge(y_ps, g * G + (t + 1))
                    dve.scalar_tensor_tensor(out=x[:, n, :], in0=ps[:, 4 + t, :], scalar=rinv1[:, t:t + 1],
                                             in1=x[:, n, :], op0=ALU.mult, op1=ALU.add).then_inc(x1_done, 1)
                    tile_stats(dve, n, g * G + (t + NT), t % 2, 1, x1_done, g * G + (t + 1))

            rows(0)
            steps(dve, NG, 1, 1, 1, lambda n, u, r: group(n))

        def attn1_tensor(pe):
            pe.wait_ge(consts, 4)

            def parts(outp, w, xx):
                last = None
                pairs = [(HI, HI), (HI, LO), (LO, HI)]
                for i, (p, q) in enumerate(pairs):
                    for t in range(DT):
                        last = pe.matmul(outp, w(p, t), xx(q, t), start=(i == 0 and t == 0),
                                         stop=(i == 2 and t == DT - 1))
                return last

            def group(g):
                for t in range(G):
                    pe.wait_ge(row_rdy, g * G + (t + 1))
                    if later(g, 1):
                        pe.wait_ge(o_rdy, (g - 1) * G + (t + 1))
                    tb = ps[:, t, :].bitcast(F16)
                    for h in range(2):
                        for e in range(DT):
                            c = (h * DT + e) * P
                            last = pe.transpose(tb[:, c:c + P], rows1[:, t, h, e * P:(e + 1) * P], ident16[:])
                    last.then_inc(t_ps, 1)
                if not later(g, 1):
                    pe.wait_ge(w_lo, 1)
                pe.wait_ge(xt_rdy, g * G + G)
                for e in range(G):
                    if later(g, 1):
                        pe.wait_ge(x1_done, (g - 1) * G + (e + 1))
                    parts(ps[:, 4 + e, :], lambda p, t: w3[:, 0, p, t, e * P:(e + 1) * P],
                          lambda q, t: xt1[:, q, t, :, :]).then_inc(q_ps, 1)
                if not later(g, 1):
                    pe.wait_ge(w_lo, 2)
                for e in range(G):
                    parts(ps[:, e, :], lambda p, t: w3[:, 1, p, t, e * P:(e + 1) * P],
                          lambda q, t: xt1[:, q, t, :, :]).then_inc(k_ps, 1)
                if not later(g, 1):
                    pe.wait_ge(w_lo, 3)
                for t in range(G):
                    pe.wait_ge(q_rdy, g * G + (t + 1))
                    parts(ps[:, 4 + t, :], lambda p, e: xt1[:, p, e, t, :],
                          lambda q, e: w3[:, 2, q, e, :]).then_inc(v_ps, 1)
                pe.wait_ge(k_rdy, g * G + G)
                pe.wait_ge(ct_in, g * (16 * G) + 16 * G)
                for t in range(G):
                    for k, keys in enumerate((ct1[:, t, :, :], kt[:, :, t, :])):
                        for e in range(DT):
                            last = pe.matmul(ps[:, t, k * P:(k + 1) * P], qt[:, e, t, :], keys[:, e, :],
                                             start=(e == 0), stop=(e == DT - 1))
                    last.then_inc(s_ps, 1)
                for t in range(G):
                    pe.wait_ge(prob_rdy, g * G + (t + 1))
                    pe.wait_ge(v_rdy, g * G + (t + 1))
                    for k in range(2):
                        last = pe.transpose(ps[:, 4 + t, k * P:(k + 1) * P], prob1[:, t, k * P:(k + 1) * P], ident[:])
                    last.then_inc(pt_ps, 1)
                pe.wait_ge(cx_in, g * 16 + 16)
                for t in range(G):
                    pe.wait_ge(pt_rdy, g * G + (t + 1))
                    for e in range(DT):
                        for k, vals in enumerate((cx1[:, t, :], v1[:, t, :])):
                            last = pe.matmul(ps[:, t, e * P:(e + 1) * P], vals[:, e * P:(e + 1) * P],
                                             probt1[:, t, k, :], start=(k == 0), stop=(k == 1))
                    last.then_inc(o_ps, 1)
                if not later(g, 1):
                    pe.wait_ge(wo_in, 16)
                for t in range(G):
                    pe.wait_ge(o_rdy, g * G + (t + 1))
                    for e in range(DT):
                        last = pe.matmul(ps[:, 4 + t, :], ot1[:, t, e, :], wo[:, e, :], start=(e == 0), stop=(e == DT - 1))
                    last.then_inc(y_ps, 1)

            steps(pe, NG, 1, 1, 1, lambda n, u, r: group(n))

        per_layer = dict(xn=NT, row_hi=NT, row=NT, t_ps=NT, xt=NT, r_ps=NT, lg=NT, wd_in=16, const=8, ex_rdy=1,
                         counts=1, pre_ps=1, routed=1, icol=6 * NT, comb=2 * NT, scat_rdy=1)
        for u in range(4):
            per_layer |= {f"scat_in{u}": 8 * NT, f"scat_out{u}": 8 * NT, f"brow_in{u}": 4 * NT,
                          f"crow_in{u}": 16 * ((JOBS + 3 - u) // 4)}
        for u in range(2):
            per_layer |= {f"row_out{u}": 8 * NT, f"gath_in{u}": 16 * NT, f"y_out{u}": 16 * ((JOBS + 1 - u) // 2)}
        for part, total in (("b", NT), ("c", JOBS)):
            per_layer |= {part + n: total for n in ("xt", "gu_ps", "t_ps", "silu", "hid", "ht_ps", "ht", "y_ps", "y")}
        msem = {n: sem("m_" + n) for n in per_layer}
        route_step = [sem(f"route_step{k}") for k in range(2)]
        odds_rdy = sem("odds_rdy")
        moe = [msem, msem]

        def wait(eng, k, name, value):
            eng.wait_ge(msem[name], k * per_layer[name] + value)

        def wait_alone(eng, k, name, value):
            wait_apart(eng, msem[name], k * per_layer[name] + value)

        hrow_t = hrow.rearrange("(n p) d -> n p d", p=P)
        xslot_t = xslot.rearrange("(n p) d -> n p d", p=P)
        yslot_t = yslot.rearrange("(n p) d -> n p d", p=P)
        out_t = out.rearrange("(n p) d -> n p d", p=P)
        out_sent = sem("out_sent")

        def rows_scalar(act, k):
            s = moe[k]

            def step(n, u, r):
                if earlier(n, NT):
                    if later(n, 2):
                        wait(act, k, "row", n - 1)
                    act.activation(xn2[:, u, :], x[:, n, :], ACT.Identity, scale=rstd[:, bass.ds(n, 1)],
                                   bias=shift[:, bass.ds(n, 1)]).then_inc(s["xn"], 1)
                if later(n, 1):
                    v = 1 - u
                    wait(act, k, "t_ps", n)
                    if later(n, 3):
                        wait(act, k, "r_ps", n - 2)
                    act.activation(xt2[:, v, :, :, :], ps[:, v, :].bitcast(F16).rearrange("p (h e s) -> p h e s", h=2, e=DT),
                                   ACT.Copy).then_inc(s["xt"], 1)

            steps(act, NT + 1, 4, 1, 2, step)

        def rows_vector(dve, k):
            s = moe[k]

            def step(n, u, r):
                if earlier(n, NT):
                    wait(dve, k, "xn", n + 1)
                    if later(n, 2):
                        wait(dve, k, "t_ps", n - 1)
                        wait(dve, k, f"row_out{u}", r * 16)
                    dve.tensor_copy(rowout[:, u, HI, :], xn2[:, u, :]).then_inc(s["row_hi"], 1)
                    wait(dve, k, "row_hi", n + 1)
                    dve.tensor_tensor(rowout[:, u, LO, :], xn2[:, u, :], rowout[:, u, HI, :],
                                      ALU.subtract).then_inc(s["row"], 1)
                if later(n, 2):
                    wait(dve, k, "r_ps", n - 1)
                    dve.tensor_scalar(lg[:, :, bass.ds(n - 2, 1)], ps[:, 2 + u, 0:E].unsqueeze(2), UNSCALE, None,
                                      ALU.mult).then_inc(s["lg"], 1)

            steps(dve, NT + 2, 4, 2, 2, step)

        def rows_tensor(pe, k):
            s = moe[k]
            pe.wait_ge(rw_step[k], DT + 2)

            def step(n, u, r):
                if earlier(n, NT):
                    wait(pe, k, "row", n + 1)
                    if later(n, 2):
                        wait(pe, k, "xt", n - 1)
                    transposes(pe, ps[:, u, :], lambda h, e: rowout[:, u, h, e * P:(e + 1) * P]).then_inc(s["t_ps"], 1)
                if later(n, 1):
                    v = 1 - u
                    wait(pe, k, "xt", n)
                    if later(n, 3):
                        wait(pe, k, "lg", n - 2)
                    three(pe, ps[:, 2 + v, 0:E], lambda p, t: xt2[:, v, p, t, :],
                          lambda q, t: rwp[:, t, q, :], DT).then_inc(s["r_ps"], 1)

            steps(pe, NT + 1, 4, 1, 2, step)

        def rows_sync(sp, k):
            s = moe[k]

            def step(n, u, r):
                wait(sp, k, "row", n + 1)
                sp.dma_start(hrow_t[n], rowout[:, u, :, :].rearrange("p h d -> p (h d)")).then_inc(s[f"row_out{u}"], 16)

            steps(sp, NT, 2, 2, 2, step)

        def transposes(pe, bank, rows):
            tb = bank.bitcast(F16)
            for h in range(2):
                for e in range(DT):
                    c = (h * DT + e) * P
                    last = pe.transpose(tb[:, c:c + P], rows(h, e), ident16[:])
            return last

        def three(pe, outp, w, xx, tiles):
            for i, (p, q) in enumerate([(HI, HI), (HI, LO), (LO, HI)]):
                for t in range(tiles):
                    last = pe.matmul(outp, w(p, t), xx(q, t), start=(i == 0 and t == 0),
                                     stop=(i == 2 and t == tiles - 1))
            return last

        def route_vector(dve, k):
            s = moe[k]
            count = 0

            def then(ins):
                nonlocal count
                count += 1
                ins.then_inc(route_step[k], 1)
                dve.wait_ge(route_step[k], count)

            def by_tile(v):
                return v.rearrange("p e n -> p n e")

            def over_experts(v):
                return v.unsqueeze(1).broadcast_to([P, E, NT])

            def over_tiles(v):
                return v.unsqueeze(2).broadcast_to([P, E, NT])

            wait(dve, k, "const", 8)
            wait(dve, k, "lg", NT)
            then(dve.memset(ones8, 1.0))
            if k == 1:
                wait(dve, k, "ex_rdy", 1)
                then(dve.tensor_scalar(lg, lg, 1.0, None, ALU.add))
                then(dve.reciprocal(lg, lg))
            for top, idx, m, cand in ((top1, idx1, m1, lg), (top2, idx2, m2, z)):
                if m is m2:
                    then(dve.scalar_tensor_tensor(out=z.rearrange("p e n -> p (e n)"), in0=m1.rearrange("p e n -> p (e n)"),
                                                  scalar=-3e38, in1=lg.rearrange("p e n -> p (e n)"),
                                                  op0=ALU.mult, op1=ALU.add))
                then(dve.tensor_reduce(top, by_tile(cand), AX.X, ALU.max))
                then(dve.tensor_tensor(m, cand, over_experts(top), ALU.is_equal))
                then(dve.tensor_tensor(m, m, em8, ALU.mult))
                then(dve.tensor_reduce(idx, by_tile(m), AX.X, ALU.min))
                then(dve.tensor_tensor(m, em8, over_experts(idx), ALU.is_equal))
            then(dve.tensor_tensor(asg, m1, m2, ALU.add))
            flat = "p e n -> p (e n)"
            then(dve.tensor_tensor_scan(cum.rearrange(flat), scanmask.rearrange(flat), asg.rearrange(flat), 0.0,
                                        ALU.mult, ALU.add))
            dve.nop().then_inc(s["counts"], 1)
            wait(dve, k, "pre_ps", 1)
            then(dve.tensor_scalar(tiles_i, ps[:, 4, E:2 * E], float(P - 1), None, ALU.add))
            then(dve.tensor_scalar(tiles_i, tiles_i, 7, None, ALU.arith_shift_right))
            then(dve.tensor_copy(tiles_f, tiles_i))
            then(dve.tensor_tensor_scan(tiles_c, ones8, tiles_f, 0.0, ALU.mult, ALU.add))
            then(dve.tensor_tensor(base, tiles_c, tiles_f, ALU.subtract))
            then(dve.scalar_tensor_tensor(out=startpos, in0=base, scalar=float(P), in1=ps[:, 4, 0:E],
                                          op0=ALU.mult, op1=ALU.add))
            then(dve.tensor_tensor(z, cum, asg, ALU.subtract))
            then(dve.tensor_tensor(z, z, over_tiles(startpos), ALU.add))
            for m, pos, idx in ((m1, pos1, idx1), (m2, pos2, idx2)):
                then(dve.tensor_tensor(m, m, z, ALU.mult))
                then(dve.tensor_reduce(idx, by_tile(m), AX.X, ALU.add))
                then(dve.tensor_copy(pos, idx))
            then(dve.memset(jexp, 0.0))
            for e in range(1, E):
                then(dve.scalar_tensor_tensor(out=jexp, in0=jidx, scalar=base[:, e:e + 1], in1=jexp,
                                              op0=ALU.is_ge, op1=ALU.add))
            then(dve.tensor_copy(eid, jexp))
            if k == 0:
                then(dve.tensor_tensor(ex, top2, top1, ALU.subtract))
                dve.nop().then_inc(odds_rdy, 1)
                wait(dve, k, "ex_rdy", 1)
                then(dve.tensor_scalar(w1, ex, 1.0, None, ALU.add))
                then(dve.reciprocal(w1, w1))
                then(dve.tensor_tensor(w2, ex, w1, ALU.mult))
                then(dve.memset(s12, UNSCALE))
            else:
                then(dve.memset(w1, 1.0))
                then(dve.memset(w2, 1.0))
                then(dve.tensor_scalar(s12[:, 0, :], top1, UNSCALE, None, ALU.mult))
                then(dve.tensor_scalar(s12[:, 1, :], top2, UNSCALE, None, ALU.mult))
            dve.nop().then_inc(s["routed"], 1)

        def route_tables(pool, k):
            s = moe[k]
            pool.iota(em8, pattern=[[1, E], [0, NT]], base=-E, channel_multiplier=0, allow_small_or_imprecise_dtypes=True).then_inc(s["const"], 1)
            pool.iota(jidx, pattern=[[1, JOBS]], base=0, channel_multiplier=0, allow_small_or_imprecise_dtypes=True).then_inc(s["const"], 1)
            pool.memset(scanmask, 1.0).then_inc(s["const"], 1)
            pool.memset(ones, 1.0).then_inc(s["const"], 1)
            pool.memset(unscale, UNSCALE).then_inc(s["const"], 1)
            pool.memset(tri, 1.0).then_inc(s["const"], 1)
            wait(pool, k, "const", 6)
            pool.memset(scanmask[:, :, 0:1], 0.0).then_inc(s["const"], 1)
            pool.affine_select(out=tri, in_=tri, compare_op=ALU.is_gt, fill=0.0, base=0,
                               pattern=[[1, P]], channel_multiplier=-1).then_inc(s["const"], 1)

        def route_tensor(pe, k):
            s = moe[k]
            wait(pe, k, "counts", 1)
            counts = cum[:, :, NT - 1:NT].rearrange("p e n -> p (e n)")
            pe.matmul(ps[:, 4, 0:E], tri, counts, start=True, stop=True)
            pe.matmul(ps[:, 4, E:2 * E], ones, counts, start=True, stop=True).then_inc(s["pre_ps"], 1)

        def scatter_gpsimd(pool, k):
            s = moe[k]
            wait(pool, k, "routed", 1)
            pool.wait_ge(zero_out, 16 * JOBS)

            def step(n, u, r):
                wait(pool, k, f"scat_in{u}", r * 32 + 32)
                if later(n, 4):
                    wait(pool, k, f"scat_out{u}", r * 32)
                one = bass.ds(n, 1)
                pool.tensor_copy(icol[:, u, 0:1], pos1[:, one]).then_inc(s["icol"], 1)
                pool.tensor_copy(icol[:, u, 1:2], pos2[:, one]).then_inc(s["icol"], 1)
                pool.tensor_copy(rowa[:, u, 2 * D:2 * D + 2].bitcast(F32), s12[:, 0, one]).then_inc(s["icol"], 1)
                pool.tensor_copy(rowb[:, u, 2 * D:2 * D + 2].bitcast(F32), s12[:, 1, one]).then_inc(s["icol"], 1)
                wait_alone(pool, k, "icol", n * 4 + 4)
                for j, buf in enumerate((rowa, rowb)):
                    pool.indirect_dma_start(out=xslot, out_offset=bass.IndirectOffsetOnAxis(ap=icol[:, u, j:j + 1], axis=0),
                                            in_=buf[:, u, :].bitcast(I32), in_offset=None).then_inc(s[f"scat_out{u}"], 16)

            steps(pool, NT, 4, 4, 4, step)
            for u in range(4):
                wait(pool, k, f"scat_out{u}", 32 * (NT // 4))
            pool.nop().then_inc(s["scat_rdy"], 1)

        def jobs_sync(sp, k, part, total):
            s = moe[k]
            src = hrow_t if part == "b" else xslot_t
            width = 2 * D if part == "b" else 2 * D + 2
            if part == "b":
                for u in range(2):
                    wait(sp, k, f"row_out{u}", 16 * (NT // 2))
            else:
                wait(sp, k, "scat_rdy", 1)
                wait(sp, k, "by", NT)

            def load(n, u, r):
                buf = rowin[:, u, 0:width]
                sp.dma_start(buf if part == "b" else buf.bitcast(I32), src[n]).then_inc(s[f"{part}row_in{u}"], 16)

            def scatter_loads(n, v, q):
                if later(n, 4):
                    wait(sp, k, f"scat_out{v}", q * 32)
                sp.dma_start(rowa[:, v, 0:2 * D], hrow_t[n]).then_inc(s[f"scat_in{v}"], 16)
                sp.dma_start(rowb[:, v, 0:2 * D], hrow_t[n]).then_inc(s[f"scat_in{v}"], 16)

            for n in range(4):
                load(n, n, 0)

            def step(n, u, r):
                if part == "b" and isinstance(n, int) and n < 4:
                    scatter_loads(n, n, 0)
                if later(n, 1) and part == "c":
                    v = (u + 1) % 2
                    wait(sp, k, "cy", n)
                    sp.dma_start(yslot_t[n - 1], yb[:, v, :]).then_inc(s[f"y_out{v}"], 16)
                if earlier(n, total - 4):
                    wait(sp, k, part + "hid", n + 1)
                    load(n + 4, u, r)

            if part == "b":
                steps(sp, NT, 4, 4, 4, lambda n, u, r: (step(n, u, r), later(n, 4) and scatter_loads(n, u, r)))
            else:
                steps(sp, total + 1, 4, 8, 4, step)

        def jobs_tensor(pe, k, part, total):
            s = moe[k]
            if part == "b":
                wait(pe, k, "wd_in", 16)
                pe.wait_ge(chunk_step, (k + 1) * 3 * CHUNKS)
            else:
                wait(pe, k, "routed", 1)
            wait(pe, k, "lg" if part == "b" else "by", NT)

            def rows_in(n, v, q):
                wait(pe, k, f"{part}row_in{v}", q * 16 + 16)
                if later(n, 2):
                    wait(pe, k, part + "xt", n - 1)
                transposes(pe, ps[:, 2 + v % 2, :], lambda h, e: rowin[:, v, h * D + e * P:h * D + (e + 1) * P]).then_inc(s[part + "t_ps"], 1)

            rows_in(0, 0, 0)

            def step(n, w, r):
                u, v = w % 2, 1 - w % 2
                if part == "c":
                    if earlier(n, total):
                        e = pe.value_load(eid[0:1, bass.ds(n, 1)], min_val=0, max_val=E - 1)
                    if later(n, 1):
                        before = pe.value_load(eid[0:1, bass.ds(n - 1, 1)], min_val=0, max_val=E - 1)
                if earlier(n, total):
                    wait(pe, k, part + "xt", n + 1)
                    if later(n, 2):
                        wait(pe, k, part + "hid", n - 1)
                    if part == "b":
                        first = lambda q, t: wgu[:, E * DT + t, q, :]
                    else:
                        first = lambda q, t: wgu[:, e * DT + t, q, :]
                    three(pe, ps[:, u, :], lambda p, t: xt2[:, u, p, t, :], first, DT).then_inc(s[part + "gu_ps"], 1)
                if earlier(n, total - 1):
                    rows_in(n + 1, (w + 1) % 4, r + (w + 1) // 4)
                if later(n, 1):
                    wait(pe, k, part + "ht", n)
                    if later(n, 3):
                        wait(pe, k, part + "y", n - 2)
                    if part == "b":
                        second = lambda f: wd[:, E, f, :]
                    else:
                        second = lambda f: wd[:, before, f, :]
                    for f in range(FT):
                        last = pe.matmul(ps[:, 6 + v, :], ht[:, v, f, :], second(f), start=(f == 0), stop=(f == FT - 1))
                    last.then_inc(s[part + "y_ps"], 1)
                if earlier(n, total):
                    wait(pe, k, part + "hid", n + 1)
                    if later(n, 2):
                        wait(pe, k, part + "ht", n - 1)
                    for f in range(FT):
                        last = pe.transpose(ps[:, 4 + u, f * P:(f + 1) * P], hid[:, u, f * P:(f + 1) * P], ident[:])
                    last.then_inc(s[part + "ht_ps"], 1)

            steps(pe, total + 1, 4, 4 + (total + 1) % 4, 4, step)

        def jobs_scalar(act, k, part, total):
            s = moe[k]

            def columns_in(n, v):
                wait(act, k, part + "t_ps", n + 1)
                if later(n, 2):
                    wait(act, k, part + "gu_ps", n - 1)
                act.activation(xt2[:, v, :, :, :], ps[:, 2 + v, :].bitcast(F16).rearrange("p (h e s) -> p h e s", h=2, e=DT),
                               ACT.Copy).then_inc(s[part + "xt"], 1)

            columns_in(0, 0)

            def step(n, w, r):
                u = w % 2
                wait(act, k, part + "gu_ps", n + 1)
                if later(n, 2):
                    wait(act, k, part + "hid", n - 1)
                scale = unscale if part == "b" else rowin[:, w, 2 * D:2 * D + 2].bitcast(F32)
                act.activation(sg[:, u, :], ps[:, u, 0:F], ACT.Silu, scale=scale).then_inc(s[part + "silu"], 1)
                if earlier(n, total - 1):
                    columns_in(n + 1, 1 - u)
                wait(act, k, part + "ht_ps", n + 1)
                if later(n, 2):
                    wait(act, k, part + "y_ps", n - 1)
                act.activation(ht[:, u, :, :], ps[:, 4 + u, 0:F].rearrange("p (f s) -> p f s", f=FT),
                               ACT.Copy).then_inc(s[part + "ht"], 1)

            steps(act, total, 4, 4 if total % 4 == 0 else total % 4, 4, step)

        def jobs_vector(dve, k, part, total):
            s = moe[k]

            def step(n, w, r):
                u, v = w % 2, 1 - w % 2
                if earlier(n, total):
                    wait(dve, k, part + "silu", n + 1)
                    if later(n, 2):
                        wait(dve, k, part + "ht_ps", n - 1)
                    scale = unscale if part == "b" else rowin[:, w, 2 * D:2 * D + 2].bitcast(F32)
                    dve.scalar_tensor_tensor(out=hid[:, u, :], in0=ps[:, u, F:2 * F], scalar=scale, in1=sg[:, u, :],
                                             op0=ALU.mult, op1=ALU.mult).then_inc(s[part + "hid"], 1)
                if later(n, 1):
                    wait(dve, k, part + "y_ps", n)
                    if part == "b":
                        dve.tensor_tensor(x[:, n - 1, :], x[:, n - 1, :], ps[:, 6 + v, :], ALU.add).then_inc(s["by"], 1)
                    else:
                        if later(n, 3):
                            wait(dve, k, f"y_out{v}", (r * 2 + (w - 1) // 2) * 16)
                        dve.tensor_copy(yb[:, v, :], ps[:, 6 + v, :]).then_inc(s["cy"], 1)

            steps(dve, total + 1, 4, 4 + (total + 1) % 4, 4, step)

        def combine_gpsimd(pool, k):
            s = moe[k]
            wait(pool, k, "y_out0", 16 * ((JOBS + 1) // 2))
            wait(pool, k, "y_out1", 16 * (JOBS // 2))

            def step(n, u, r):
                if later(n, 2):
                    wait(pool, k, "comb", n * 2 - 2)
                one = bass.ds(n, 1)
                pool.tensor_copy(icol[:, u, 0:1], pos1[:, one]).then_inc(s["icol"], 1)
                pool.tensor_copy(icol[:, u, 1:2], pos2[:, one]).then_inc(s["icol"], 1)
                wait_alone(pool, k, "icol", n * 2 + (4 * NT + 2))
                for j in range(2):
                    pool.indirect_dma_start(out=gy[:, u, j, :], out_offset=None, in_=yslot,
                                            in_offset=bass.IndirectOffsetOnAxis(ap=icol[:, u, j:j + 1], axis=0)
                                            ).then_inc(s[f"gath_in{u}"], 16)

            steps(pool, NT, 2, 2, 2, step)

        def combine_vector(dve, k):
            s = moe[k]

            def step(n, u, r):
                wait(dve, k, f"gath_in{u}", r * 32 + 32)
                for j, w in enumerate((w1, w2)):
                    dve.scalar_tensor_tensor(out=x[:, n, :], in0=gy[:, u, j, :], scalar=w[:, bass.ds(n, 1)],
                                             in1=x[:, n, :], op0=ALU.mult, op1=ALU.add).then_inc(s["comb"], 1)
                    if j == 0:
                        wait(dve, k, "comb", n * 2 + 1)
                if k == 0:
                    tile_stats(dve, n, n + 2 * NT, u, 2, s["comb"], n * 2 + 2)

            steps(dve, NT, 2, 2, 2, step)

        def combine_sync(sp, k):
            def step(n, u, r):
                wait(sp, k, "comb", n * 2 + 2)
                sp.dma_start(out_t[n], x[:, n, :]).then_inc(out_sent, 16)

            steps(sp, NT, 2, 2, 2, step)
            sp.wait_ge(out_sent, 16 * NT)

        def moe_sync(sp, k):
            s = moe[k]
            sp.wait_ge(stats_rdy[2 * k + 1], NT)
            sp.dma_start(wd, a[f"L{k}_d"].rearrange("e (f p) n -> p e f n", p=P)).then_inc(s["wd_in"], 16)
            rows_sync(sp, k)
            jobs_sync(sp, k, "b", NT)
            jobs_sync(sp, k, "c", JOBS)
            if k == 1:
                combine_sync(sp, k)

        def moe_gpsimd(pool, k):
            norm_factors(2 * k + 1, XS, k == 0)
            route_tables(pool, k)
            scatter_gpsimd(pool, k)
            combine_gpsimd(pool, k)

        def moe_scalar(act, k):
            s = moe[k]
            act.wait_ge(factors[2 * k + 1], FACTOR_STEPS[k == 0])
            rows_scalar(act, k)
            if k == 1:
                wait(act, k, "lg", NT)
                act.activation(lg, lg, ACT.Exp, scale=-1.0).then_inc(s["ex_rdy"], 1)
            else:
                act.wait_ge(odds_rdy, 1)
                act.activation(ex, ex, ACT.Exp).then_inc(s["ex_rdy"], 1)
            wait(act, k, "const", 8)
            jobs_scalar(act, k, "b", NT)
            jobs_scalar(act, k, "c", JOBS)

        def moe_vector(dve, k):
            rows_vector(dve, k)
            route_vector(dve, k)
            jobs_vector(dve, k, "b", NT)
            jobs_vector(dve, k, "c", JOBS)
            combine_vector(dve, k)

        def moe_tensor(pe, k):
            rows_tensor(pe, k)
            pe.wait_ge(moe[k]["const"], 8)
            route_tensor(pe, k)
            jobs_tensor(pe, k, "b", NT)
            jobs_tensor(pe, k, "c", JOBS)

        stack_in = [sem(f"stack_in{u}") for u in range(4)]
        qn_rdy, qp_step, qp_rdy, qst_out = sem("qn_rdy"), sem("qp_step"), sem("qp_rdy"), sem("qst_out")
        s3_ps, max3_rdy, mt_ps, nm_step, nm_rdy, maxrow_in = [sem(n) for n in (
            "s3_ps", "max3_rdy", "mt_ps", "nm_step", "nm_rdy", "maxrow_in")]
        st_ps, exp_rdy, pv_ps, osb_rdy, rden_rdy, att_step, x3_done = [sem(n) for n in (
            "st_ps", "exp_rdy", "pv_ps", "osb_rdy", "rden_rdy", "att_step", "x3_done")]
        align_in = [sem(f"align_in{w}") for w in range(2)]
        ct3_in, va_rdy, ones_set = sem("ct3_in"), sem("va_rdy"), sem("ones_set")
        ALIGN = 16 * 8
        STACKED = 16 * SLOTS

        def attn2_sync(sp):
            sp.wait_ge(stats_rdy[2], NT)
            sp.wait_ge(kp_out, STACKED * NT)
            ctT = a["ctxT"].rearrange("b (e p) s -> b p e s", p=P)

            def parts_out(b, v):
                wait_apart(sp, qp_rdy, b + 1)
                for s, part in enumerate(Q_PARTS):
                    sp.dma_start(qst[v, s * HD:(s + 1) * HD].rearrange("d h m -> h d m"), qparts[:, part, :]).then_inc(qst_out, 16)

            def load(b, half, slot, v):
                sp.wait_ge(qst_out, b * STACKED + STACKED)
                sp.dma_start(ks[0:KR, slot, :, :], kst[b, :, 4 * half:4 * half + 4, :]).then_inc(stack_in[slot], 16)
                sp.dma_start(qs[0:KR, slot, :, :], qst[v, :, 4 * half:4 * half + 4, :]).then_inc(stack_in[slot], 16)

            def columns(b, v):
                sp.dma_start(ct3[:, v, :, :], ctT[b]).then_inc(ct3_in, 16)

            def max_rows(q, u):
                sp.wait_ge(nm_rdy, q + 1)
                for j in range(MAX_PARTS):
                    sp.dma_start(qs[KR + j:KR + j + 1, u, :, :], nm[0:16, j, :]).then_inc(maxrow_in, 16)

            sp.dma_start(rw[:], a["L1_rw"]).then_inc(rw_in[1], 16)
            columns(0, 0)
            parts_out(0, 0)
            load(0, 0, 0, 0)
            load(0, 1, 1, 0)
            parts_out(1, 1)
            load(1, 0, 2, 1)
            max_rows(0, 0)

            def step(q, u, r):
                b, v = r * 2 + u // 2, u // 2
                if u % 2 == 0 and earlier(q, QUADS - 2):
                    if later(q, 2):
                        sp.wait_ge(va_rdy, b)
                    columns(b + 1, 1 - v)
                if earlier(q, QUADS - 3):
                    if later(q, 1):
                        sp.wait_ge(st_ps, q * 16)
                    load(r * 2 + (u + 3) // 2, (u + 1) % 2, (u + 3) % 4, ((u + 3) // 2) % 2)
                if earlier(q, QUADS - 1):
                    max_rows(q + 1, (u + 1) % 4)
                if later(q, 1) and earlier(q, QUADS + 1):
                    wait_apart(sp, osb_rdy, q)
                    w, row, bv = (u + 1) % 2, 64 * ((u + 1) % 2), ((u + 3) % 4) // 2
                    if w == 0 and later(q, 5):
                        sp.wait_ge(x3_done, b - 1)
                    for h in range(4):
                        sp.dma_start(num[row + h * HD:row + (h + 1) * HD, bv, :], osb[32 * h:32 * h + HD, w, :]).then_inc(align_in[w], 16)
                        sp.dma_start(den[row + h * HD:row + (h + 1) * HD, bv, :], osb[32 * h + HD:32 * h + 2 * HD, w, :]).then_inc(align_in[w], 16)
                if u % 2 == 0 and earlier(q, QUADS - 4):
                    loaded = r * 32 + 32 if isinstance(r, int) else sp.snap(r * 32 + 32)
                    wait_apart(sp, stack_in[2 * v], loaded)
                    wait_apart(sp, stack_in[2 * v + 1], loaded)
                    parts_out(b + 2, v)
                if u % 2 == 0 and later(q, 4) and earlier(q, QUADS - 4):
                    for j in range(3):
                        load_chunk(sp, 1, stage3[:, j, :], b * 3 + (j - 6), j, b - 2)

            steps(sp, QUADS + 4, 4, 8, 4, step)

        def attn2_gpsimd(pool):
            norm_factors(2, 1.0, False)
            pool.memset(ks[KR:KM, :, :, :], 1.0).then_inc(ones_set, 1)
            pool.wait_ge(ones_set, 1)
            pool.memset(va[:, :, :, :, HD:2 * HD], 1.0).then_inc(ones_set, 1)

            def parts(b):
                pool.wait_ge(qn_rdy, b + 1)
                if later(b, 1):
                    wait_apart(pool, qst_out, b * STACKED)
                n = b * 4
                pool.tensor_scalar(qparts[:, 0, :], qn, 1.0, 1.0, ALU.mult, ALU.mult).then_inc(qp_step, 1)
                wait_apart(pool, qp_step, n + 1)
                pool.tensor_tensor(qn, qn, qparts[:, 0, :], ALU.subtract).then_inc(qp_step, 1)
                wait_apart(pool, qp_step, n + 2)
                pool.tensor_scalar(qparts[:, 1, :], qn, 1.0, 1.0, ALU.mult, ALU.mult).then_inc(qp_step, 1)
                wait_apart(pool, qp_step, n + 3)
                pool.tensor_tensor(qparts[:, 2, :], qn, qparts[:, 1, :], ALU.subtract).then_inc(qp_step, 1)
                pool.wait_ge(qp_step, n + 4)
                pool.nop().then_inc(qp_rdy, 1)

            def values(b, v):
                wait_apart(pool, ct3_in, b * 16 + 16)
                if later(b, 2):
                    wait_apart(pool, pv_ps, b * 8 - 8)
                pool.tensor_copy(va[:, v, :, :, 0:HD], ct3[:, v, :, :].rearrange("p e (h d) -> p e h d", h=H)).then_inc(va_rdy, 1)

            parts(0)
            values(0, 0)
            parts(1)

            def step(q, u, r):
                b, v = r * 2 + u // 2, u // 2
                if u % 2 == 0:
                    if earlier(q, QUADS - 4):
                        parts(b + 2)
                    if earlier(q, QUADS - 2):
                        values(b + 1, 1 - v)
                    if later(q, 4) and earlier(q, QUADS - 4):
                        for j in range(3):
                            prepare_chunk(1, stage3[:, j, :], b * 3 + (j - 6), j, b - 2, j)
                elif later(q, 3) and earlier(q, QUADS + 2):
                    pool.wait_ge(rden_rdy, b * DT)
                    pool.tensor_tensor(num[:, 1 - v, :], num[:, 1 - v, :], den[:, 1 - v, :], ALU.mult).then_inc(att_step, 1)
                    wait_apart(pool, att_step, b)
                    pool.tensor_tensor(x[:, b - 1, :], x[:, b - 1, :], num[:, 1 - v, :], ALU.add).then_inc(x3_done, 1)

            steps(pool, QUADS + 4, 4, 8, 4, step)
            pool.wait_ge(stats_rdy[3], NT)
            prepare_router(1)

        def attn2_scalar(act):
            act.wait_ge(factors[2], FACTOR_STEPS[False])

            def normed(b):
                if later(b, 1):
                    act.wait_ge(qp_step, b * 4)
                one = bass.ds(b, 1)
                act.activation(qn, x[:, b, :], ACT.Identity, scale=rstd[:, one], bias=shift[:, one]).then_inc(qn_rdy, 1)

            normed(0)
            normed(1)

            def results_out(q, w, moved):
                act.wait_ge(pv_ps, q * 4 + 4)
                if later(q, 2):
                    act.wait_ge(align_in[w], moved * ALIGN)
                act.activation(osb[:, w, :], ps[:, 6, :], ACT.Copy).then_inc(osb_rdy, 1)

            def step(q, u, r):
                for e in range(DT):
                    if later(q, 1) or e >= 2:
                        act.wait_ge(pv_ps, q * 4 + (e - 1))
                    for h in range(4):
                        n = 4 * e + h
                        act.wait_ge(st_ps, q * 16 + (n + 1))
                        act.activation(prob3[:, e % 2, h, :], ps[:, 4 + n % 2, :], ACT.Exp, scale=HEAD_SCORE).then_inc(exp_rdy, 1)
                    if e == 0 and later(q, 1):
                        results_out(q - 1, (u + 1) % 2, r * 2 + (u - 1) // 2)
                    if e == 2 and u % 2 == 0 and earlier(q, QUADS - 4):
                        normed(r * 2 + (u // 2 + 2))

            steps(act, QUADS, 4, 4, 4, step)
            results_out(QUADS - 1, 1, NT - 1)

        def attn2_vector(dve):
            def maxima(q, v, between):
                if later(q, 2):
                    dve.wait_ge(mt_ps, q - 1)
                for n in range(8):
                    dve.wait_ge(s3_ps, q * 8 + (n + 1))
                    dve.tensor_reduce(mx[:, v, 2 * n:2 * n + 2], ps[:, 2 * (n % 2):2 * (n % 2) + 2, :], AX.X, ALU.max,
                                      negate=True).then_inc(max3_rdy, 1)
                    between.get(n, lambda: None)()

            def max_parts(q):
                dve.wait_ge(mt_ps, q + 1)
                if later(q, 1):
                    dve.wait_ge(maxrow_in, q * (16 * MAX_PARTS))
                m = ps[0:16, 7, 0:P]
                dve.tensor_copy(nm[0:16, 0, :], m).then_inc(nm_step, 1)
                dve.wait_ge(nm_step, q + 1)
                dve.tensor_tensor(nm[0:16, 1, :], m, nm[0:16, 0, :], ALU.subtract).then_inc(nm_rdy, 1)

            maxima(0, 0, {})
            max_parts(0)
            maxima(1, 1, {})

            def step(q, u, r):
                b, v = r * 2 + u // 2, u // 2
                todo = {}
                if earlier(q, QUADS - 1):
                    todo[2] = lambda: max_parts(q + 1)
                if u % 2 == 1 and later(q, 3) and earlier(q, QUADS + 2):
                    def one_over_sums(i):
                        if i == 0:
                            for w in range(2):
                                dve.wait_ge(align_in[w], b * ALIGN)
                        part = den[:, 1 - v, i * P:(i + 1) * P]
                        dve.reciprocal(part, part).then_inc(rden_rdy, 1)
                    for i in range(DT):
                        todo[4 + i] = lambda i=i: one_over_sums(i)
                if u % 2 == 0 and later(q, 4):
                    todo[5] = lambda: tile_stats(dve, b - 2, b + (3 * NT - 2), v, 3, x3_done, b - 1)
                if earlier(q, QUADS - 2):
                    maxima(q + 2, u % 2, todo)
                else:
                    for n in sorted(todo):
                        todo[n]()

            steps(dve, QUADS + 4, 4, 8, 4, step)

        def attn2_tensor(pe):
            pe.wait_ge(ones_set, 2)

            def maxima(q, slot, r, n):
                if n == 0:
                    pe.wait_ge(stack_in[slot], r * 32 + 32)
                if later(q, 1) or n >= 2:
                    pe.wait_ge(max3_rdy, q * 8 + (n - 1))
                for m in (2 * (n % 2), 2 * (n % 2) + 1):
                    last = pe.matmul(ps[:, m, :], qs[0:KR, slot, n // 2, m * P:(m + 1) * P], ks[0:KR, slot, n // 2, :],
                                     start=True, stop=True)
                last.then_inc(s3_ps, 1)

            def turn_maxima(q, v):
                pe.wait_ge(max3_rdy, q * 8 + 8)
                if later(q, 1):
                    pe.wait_ge(nm_rdy, q)
                pe.transpose(ps[0:16, 7, 0:P], mx[:, v, :], ident[:]).then_inc(mt_ps, 1)

            def products(q, e, half, v, b):
                pe.wait_ge(exp_rdy, q * 16 + (4 * e + 4))
                if e == 0:
                    pe.wait_ge(va_rdy, b + 1)
                    if later(q, 1):
                        pe.wait_ge(osb_rdy, q)
                for h in range(4):
                    last = pe.matmul(ps[2 * HD * h:2 * HD * (h + 1), 6, :], va[:, v, e, 4 * half + h, :],
                                     prob3[:, e % 2, h, :], start=(e == 0), stop=(e == DT - 1))
                last.then_inc(pv_ps, 1)

            for q in range(2):
                for n in range(8):
                    maxima(q, q, 0, n)
                if q == 0:
                    turn_maxima(0, 0)

            def step(q, u, r):
                b = r * 2 + u // 2
                before = (u + 3) % 4
                pe.wait_ge(maxrow_in, q * (16 * MAX_PARTS) + 16 * MAX_PARTS)
                for e in range(DT):
                    def scores(h):
                        n = 4 * e + h
                        if later(q, 1) or n >= 2:
                            pe.wait_ge(exp_rdy, q * 16 + (n - 1))
                        pe.matmul(ps[:, 4 + n % 2, :], ks[0:KM, u, h, e * P:(e + 1) * P], qs[0:KM, u, h, :],
                                  start=True, stop=True).then_inc(st_ps, 1)

                    def next_maxima(half):
                        if earlier(q, QUADS - 2):
                            maxima(q + 2, (u + 2) % 4, r + (u + 2) // 4, 2 * e + half)

                    scores(0)
                    scores(1)
                    next_maxima(0)
                    scores(2)
                    if e >= 1:
                        products(q, e - 1, u % 2, u // 2, b)
                    elif later(q, 1):
                        products(q - 1, DT - 1, before % 2, before // 2, b)
                    scores(3)
                    if e == 1 and earlier(q, QUADS - 1):
                        turn_maxima(q + 1, (u + 1) % 2)
                    next_maxima(1)

            steps(pe, QUADS, 4, 4, 4, step)
            products(QUADS - 1, DT - 1, 1, 1, NT - 1)

        block = ctx.enter_context(nc.Block())

        @block.sync
        def _(sp):
            attn1_sync(sp)
            moe_sync(sp, 0)
            attn2_sync(sp)
            moe_sync(sp, 1)

        @block.gpsimd
        def _(pool):
            attn1_gpsimd(pool)
            moe_gpsimd(pool, 0)
            attn2_gpsimd(pool)
            moe_gpsimd(pool, 1)

        @block.scalar
        def _(act):
            attn1_scalar(act)
            moe_scalar(act, 0)
            attn2_scalar(act)
            moe_scalar(act, 1)

        @block.vector
        def _(dve):
            attn1_vector(dve)
            moe_vector(dve, 0)
            attn2_vector(dve)
            moe_vector(dve, 1)

        @block.tensor
        def _(pe):
            attn1_tensor(pe)
            moe_tensor(pe, 0)
            attn2_tensor(pe)
            moe_tensor(pe, 1)


def kernel(x, ctx_2048, mask_BxSx4224_bf0, L0_xattn_wq, L0_xattn_wk, L0_xattn_wv, L0_xattn_wo,
           L0_ffn_rms_weight, L0_ffn_router_w, L0_ffn_w_gate, L0_ffn_w_up, L0_ffn_w_down,
           L0_ffn_sw_gate, L0_ffn_sw_up, L0_ffn_sw_down, L1_ffn_gate_w, L1_ffn_w1, L1_ffn_w2, L1_ffn_w3,
           L1_ffn_ws1, L1_ffn_ws2, L1_ffn_ws3):
    import numpy as _np
    import concourse.bacc as _bacc
    from concourse import mybir as _mybir
    from concourse.bass_utils import run_bass_kernel_spmd as _run

    def first(gate, up, s_gate, s_up):
        w = _np.concatenate([_np.concatenate([gate, s_gate[None]]), _np.concatenate([up, s_up[None]])], axis=2)
        return w.reshape(CHUNKS, P, 2 * F)

    def flip(w):
        return _np.asarray(w).transpose(0, 2, 1)

    def n(v):
        return _np.asarray(v)

    arrays = {
        "x": n(x).reshape(T, D),
        "ctx": n(ctx_2048).reshape(T, D),
        "ctxT": n(ctx_2048).transpose(0, 2, 1),
        "wqT": n(L0_xattn_wq).T, "wkT": n(L0_xattn_wk).T, "wvT": n(L0_xattn_wv).T, "woT": n(L0_xattn_wo).T,
        "rms": _np.tile(n(L0_ffn_rms_weight).reshape(DT, P).T, (1, NE)),
        "L0_rw": n(L0_ffn_router_w).reshape(DT, P, E).transpose(1, 0, 2),
        "L1_rw": n(L1_ffn_gate_w).T.reshape(DT, P, E).transpose(1, 0, 2),
        "L0_gu": first(n(L0_ffn_w_gate), n(L0_ffn_w_up), n(L0_ffn_sw_gate), n(L0_ffn_sw_up)),
        "L0_d": _np.concatenate([n(L0_ffn_w_down), n(L0_ffn_sw_down)[None]]),
        "L1_gu": first(flip(L1_ffn_w1), flip(L1_ffn_w3), n(L1_ffn_ws1).T, n(L1_ffn_ws3).T),
        "L1_d": _np.concatenate([flip(L1_ffn_w2), n(L1_ffn_ws2).T[None]]),
    }
    arrays = {k: _np.ascontiguousarray(v) for k, v in arrays.items()}
    nc = _bacc.Bacc("TRN2", target_bir_lowering=False, num_devices=1)
    aps = {k: nc.dram_tensor("in_" + k, v.shape, _mybir.dt.from_np(v.dtype), kind="ExternalInput").ap()
           for k, v in arrays.items()}
    out = nc.dram_tensor("out_0", (T, D), _mybir.dt.float32, kind="ExternalOutput").ap()
    build(nc, aps, out)
    r = _run(nc, [{"in_" + k: v for k, v in arrays.items()}], core_ids=[0])
    return r.results[0]["out_0"].reshape(B, P, D)
```

```python
from contextlib import ExitStack

import numpy as np
import concourse.bass as bass
from concourse import mybir

F32 = mybir.dt.float32
F16 = mybir.dt.float16
BF16 = mybir.dt.bfloat16
I32 = mybir.dt.int32
ALU = mybir.AluOpType
ACT = mybir.ActivationFunctionType
AX = mybir.AxisListType

P = 128
D = 512
DT = D // P
B = 16
T = B * P
NT = T // P
G = 4
NG = NT // G
E = 8
NE = E + 1
F = 256
FT = F // P
JOBS = 2 * T // P + E - 1
H = 8
HD = P // H
SLOTS = 6
KR = SLOTS * HD
MAX_PARTS = 2
KM = KR + MAX_PARTS
K_PARTS = (0, 1, 2, 0, 1, 0)
Q_PARTS = (0, 0, 0, 1, 1, 2)
STACKED = 16 * SLOTS
QUADS = NT * 2
CHUNKS = NE * DT
CPG = CHUNKS // NG
assert CPG == 2 * G + 1

XS = 1024.0
WS = 256.0
UNSCALE = 1.0 / (XS * WS)
SCORE = float(D) ** -0.5
HEAD_SCORE = float(HD) ** -0.5
HI, LO = 0, 1


def build(nc, a, out):
    ctx = ExitStack()
    with ctx:
        def sem(name):
            return ctx.enter_context(nc.semaphore(name))

        def sb(name, shape, dt):
            return ctx.enter_context(nc.sbuf_tensor("sb_" + name, shape, dt))

        x = sb("x", [P, NT, D], F32)
        wgu = sb("wgu", [P, CHUNKS, 2, 2 * F], F16)
        ident = sb("ident", [P, P], F32)
        ident16 = sb("ident16", [P, P], F16)
        stats = sb("stats", [P, 2, 6], F32)
        mvt = sb("mvt", [P, 2, 2], F32)
        mv = sb("mv", [P, NT, 2], F32)
        rstd = sb("rstd", [P, NT], F32)
        shift = sb("shift", [P, NT], F32)
        lnt = sb("lnt", [P, NT], F32)
        mhalf = sb("mhalf", [P, NT], F32)
        wsc = sb("wsc", [P, 2, CHUNKS], F32)
        rw = sb("rw", [P, DT, E], F32)
        rwp = sb("rwp", [P, DT, 2, E], F16)
        ps = ctx.enter_context(nc.psum_tensor("ps", [P, 8, 512], F32))

        WORDS = 25870
        pool_mem = sb("shared", [P, WORDS], F32)

        class Carve:
            def __init__(self):
                self.at = 0

            def __call__(self, shape, dt):
                n = int(np.prod(shape))
                words = n if dt in (F32, I32) else (n + 1) // 2
                v = pool_mem[:, self.at:self.at + words]
                self.at += words
                assert self.at <= WORDS, self.at
                if dt != F32:
                    v = v.bitcast(dt)
                names = " ".join("abcd"[:len(shape)])
                sizes = {"abcd"[i]: s for i, s in enumerate(shape)}
                return v.rearrange(f"p ({names}) -> p {names}", **sizes) if len(shape) > 1 else v

        kst = nc.dram_tensor("kst", [B, KR, H, D], BF16).ap()
        qst = nc.dram_tensor("qst", [2, KR, H, D], BF16).ap()
        rsum = nc.dram_tensor("rsum", [2, H, D], F32).ap()
        hrow = nc.dram_tensor("hrow", [T, 2 * D], F16).ap()
        xslot = nc.dram_tensor("xslot", [JOBS * P, D + 1], I32).ap()
        yslot = nc.dram_tensor("yslot", [JOBS * P, D], F32).ap()

        c1 = Carve()
        w3 = c1([3, 2, DT, D], F16)
        wo = c1([DT, D], F32)
        rows1 = c1([G, 2, D], F16)
        xt1_words = c1.at
        xt1 = c1([2, DT, G, P], F16)
        xn1 = c1([D], F32)
        qt_at = c1.at
        qt = c1([DT, G, P], F32)
        kt_at = c1.at
        kt = c1([DT, G, P], F32)
        v1 = c1([G, D], F32)
        ct1 = c1([G, DT, P], F32)
        cx1 = c1([G, D], F32)
        kparts = c1([3, D], BF16)
        krest = c1([D], F32)
        stage = c1([3, D], F32)
        zeros = wgu[:, 20:22, :, :].rearrange("p c h f -> p (c h f)")[:, 0:2 * D + 2]
        small1 = c1([3, G], F32)
        negmax1, rowsum1, rinv1 = small1[:, 0, :], small1[:, 1, :], small1[:, 2, :]
        prob1 = pool_mem[:, xt1_words:xt1_words + G * 256].rearrange("p (g k) -> p g k", g=G)
        probt1 = pool_mem[:, kt_at:kt_at + G * 256].rearrange("p (g k q) -> p g k q", g=G, k=2)
        ot1 = pool_mem[:, qt_at:qt_at + G * D].rearrange("p (g e q) -> p g e q", g=G, e=DT)
        wstage = [wgu[:, CHUNKS - 4 * (j + 1):CHUNKS - 4 * j, :, :].rearrange("p c h f -> p (c h f)")
                  .bitcast(F32).rearrange("p (t n) -> p t n", t=DT) for j in range(3)]

        c2 = Carve()
        wd = c2([NE, FT, D], F32)
        rowout = c2([2, 2, D], F16)
        xn2 = c2([2, D], F32)
        xt2 = c2([2, 2, DT, P], F16)
        gathered_at = c2.at
        gy = pool_mem[:, c2.at:c2.at + 8 * D].rearrange("p (u j d) -> p u j d", u=4, j=2)
        rowa = c2([4, 2 * D + 2], F16)
        rowb = c2([4, 2 * D + 2], F16)
        rowin = c2([4, 2 * D + 2], F16)
        sg = c2([2, F], F32)
        hid = c2([2, F], F32)
        ht = c2([2, FT, P], F32)
        yb = c2([2, D], F32)
        lg, m1, m2, asg, cum, z, em8, scanmask = [c2([E, NT], F32) for _ in range(8)]
        top1, top2, idx1, idx2, w1, w2, ex = [c2([NT], F32) for _ in range(7)]
        pos = c2([NT, 2], I32)
        pos1, pos2 = pos[:, :, 0], pos[:, :, 1]
        s12 = c2([2, NT], F32)
        tiles_i = c2([E], I32)
        tiles_f, tiles_c, base, ones8, startpos = [c2([E], F32) for _ in range(5)]
        jidx, jexp = c2([JOBS], F32), c2([JOBS], F32)
        eid = c2([JOBS], I32)
        tri = c2([P], F32)
        ones = c2([P], F32)
        icol = c2([4, 2], I32)
        unscale = c2([1], F32)

        c3 = Carve()
        ks = c3([4, 4, D], BF16)
        qs = c3([4, 4, D], BF16)
        qn = c3([D], F32)
        qparts = c3([3, D], BF16)
        stage3 = c3([3, D], F32)
        mx = c3([2, 16], F32)
        nm = c3([MAX_PARTS, P], BF16)
        osb = c3([2, D], F32)
        c3.at = max(c3.at, gathered_at)
        prob3 = c3([2, 4, D], F32)
        va = c3([2, DT, H, 2 * HD], F32)
        ct3 = c3([2, DT, P], F32)
        num = c3([2, D], F32)
        den = c3([2, D], F32)
        sums = c3([2, D // HD], F32)

        consts, mhalf_set, zero_set, zero_out = sem("consts"), sem("mhalf_set"), sem("zero_set"), sem("zero_out")
        x_in = [sem(f"x_in{g}") for g in range(NG)]
        w_in = [sem(f"w_in{j}") for j in range(3)]
        wo_in, rms_in, scales = sem("wo_in"), sem("rms_in"), sem("scales")
        w_hi, w_lo = sem("w_hi"), sem("w_lo")
        stat_step, stats_rdy = sem("stat_step"), [sem(f"stats_rdy{k}") for k in range(4)]
        factors = [sem(f"factors{k}") for k in range(4)]
        rw_in, rw_step = [sem(f"rw_in{k}") for k in range(2)], [sem(f"rw_step{k}") for k in range(2)]

        xn_rdy, hi_rdy, row_rdy = sem("xn_rdy"), sem("hi_rdy"), sem("row_rdy")
        t_ps, xt_rdy = sem("t_ps"), sem("xt_rdy")
        q_ps, q_rdy = sem("q_ps"), sem("q_rdy")
        k_ps, k_rdy = sem("k_ps"), sem("k_rdy")
        v_ps, v_rdy = sem("v_ps"), sem("v_rdy")
        s_ps, max_rdy, prob_rdy = sem("s_ps"), sem("max_rdy"), sem("prob_rdy")
        pt_ps, pt_rdy = sem("pt_ps"), sem("pt_rdy")
        o_ps, o_rdy = sem("o_ps"), sem("o_rdy")
        y_ps, rinv_rdy, x1_done = sem("y_ps"), sem("rinv_rdy"), sem("x1_done")
        ct_in, cx_in = sem("ct_in"), sem("cx_in")
        kp_step, kp_rdy, kp_out = sem("kp_step"), sem("kp_rdy"), sem("kp_out")
        chunk_in = [[sem(f"chunk_in{k}_{u}") for u in range(3)] for k in range(2)]
        gu_hi, gu_lo = sem("gu_hi"), sem("gu_lo")
        chunk_step = sem("chunk_step")
        AHEAD = 9

        held = sem("held")

        def wait_apart(eng, what, value):
            eng.wait_ge(what, value)
            if not isinstance(value, int):
                eng.nop().then_inc(held, 1)

        def later(n, least):
            return not isinstance(n, int) or n >= least

        def earlier(n, bound):
            return not isinstance(n, int) or n < bound

        def steps(eng, total, head, tail, unroll, step):
            assert head % unroll == 0 and (total - head - tail) % unroll == 0
            for n in range(head):
                step(n, n % unroll, n // unroll)
            with eng.Fori(0, (total - head - tail) // unroll) as i:
                for u in range(unroll):
                    step(i * unroll + (head + u), u, i + head // unroll)
            for n in range(total - tail, total):
                step(n, n % unroll, n // unroll)

        def stat_steps(dve, n, done, u, k, after=None, count=None):
            def sums():
                if after is not None:
                    wait_apart(dve, after, count)
                dve.bn_stats(stats[:, u, :], x[:, n, :]).then_inc(stat_step, 1)

            def mean_and_variance():
                wait_apart(dve, stat_step, done * 2 + 1)
                dve.bn_aggr(mvt[:, u, :], stats[:, u, :]).then_inc(stat_step, 1)

            def to_place():
                wait_apart(dve, stat_step, done * 2 + 2)
                dve.tensor_copy(mv[:, n, :], mvt[:, u, :]).then_inc(stats_rdy[k], 1)

            return sums, mean_and_variance, to_place

        def tile_stats(*which):
            for step in stat_steps(*which):
                step()

        FACTOR_STEPS = 5
        factor_steps = [0] * 4

        def norm_factors(k, scale, rms, first, end):
            pool = nc.gpsimd
            pool.wait_ge(stats_rdy[k], end)
            tiles = slice(first, end)
            n = factor_steps[k]

            def then(ins):
                nonlocal n
                n += 1
                ins.then_inc(factors[k], 1)
                pool.wait_ge(factors[k], n)

            var, mean = mv[:, tiles, 1], mv[:, tiles, 0]
            rest, r, s = lnt[:, tiles], rstd[:, tiles], shift[:, tiles]
            eps, rms_eps = 1e-5, 1e-6
            then(pool.tensor_scalar(rest, var, 1.0 + rms_eps if rms else 1.0, rms_eps * eps if rms else eps,
                                    ALU.mult, ALU.add))
            then(pool.tensor_tensor(r, rest, mhalf[:, tiles], ALU.pow))
            then(pool.tensor_scalar(r, r, scale, 1.0, ALU.mult, ALU.mult))
            then(pool.tensor_tensor(rest, mean, r, ALU.mult))
            then(pool.tensor_scalar(s, rest, -1.0, 1.0, ALU.mult, ALU.mult))
            assert n == factor_steps[k] + FACTOR_STEPS
            factor_steps[k] = n

        def load_chunk(sp, k, buf, c, u, r):
            if later(c, 3):
                if k == 0:
                    sp.wait_ge(gu_lo, c - 2)
                else:
                    sp.wait_ge(chunk_step, c * 3 + (AHEAD - 6))
            sp.dma_start(buf, a[f"L{k}_gu"][c]).then_inc(chunk_in[k][u], 16)

        def prepare_router(k):
            pool = nc.gpsimd
            pool.wait_ge(rw_in[k], 16)
            for t in range(DT):
                pool.tensor_scalar(rw[:, t, :], rw[:, t, :], wsc[:, k, t:t + 1], 1.0, ALU.mult, ALU.mult).then_inc(rw_step[k], 1)
            pool.wait_ge(rw_step[k], DT)
            pool.tensor_scalar(rwp[:, :, HI, :], rw[:], 1.0, 1.0, ALU.mult, ALU.mult).then_inc(rw_step[k], 1)
            pool.wait_ge(rw_step[k], DT + 1)
            pool.tensor_tensor(rwp[:, :, LO, :], rw[:], rwp[:, :, HI, :], ALU.subtract).then_inc(rw_step[k], 1)

        def attn1_sync(sp):
            xg = a["x"].rearrange("(g t p) d -> g p t d", t=G, p=P)
            for g in range(NG):
                sp.dma_start(x[:, g * G:(g + 1) * G, :], xg[g]).then_inc(x_in[g], 16)
                if g < 3:
                    sp.dma_start(wstage[g], a[("wqT", "wkT", "wvT")[g]].rearrange("(t p) n -> p t n", p=P)).then_inc(w_in[g], 16)
            sp.dma_start(wsc[:, 0, :], a["rms"]).then_inc(rms_in, 16)
            sp.dma_start(rw[:], a["L0_rw"]).then_inc(rw_in[0], 16)
            sp.dma_start(wo, a["woT"].rearrange("(t p) n -> p t n", p=P)).then_inc(wo_in, 16)
            ctT = a["ctxT"].rearrange("b (e p) s -> b p e s", p=P)
            cx = a["ctx"].rearrange("(g t p) d -> g p t d", t=G, p=P)

            def context(g):
                for t in range(G):
                    sp.dma_start(ct1[:, t, :, :], ctT[g * G + t]).then_inc(ct_in, 16)
                sp.dma_start(cx1, cx[g]).then_inc(cx_in, 16)

            context(0)
            xz = xslot.rearrange("(j p) n -> j p n", p=P)

            def clear_slots(first, end):
                sp.wait_ge(zero_set, 1)
                with sp.Fori(first, end) as j:
                    sp.dma_start(xz[j], zeros.bitcast(I32)).then_inc(zero_out, 16)

            def group(g):
                def chunks(js):
                    for j in js:
                        load_chunk(sp, 0, stage[:, j % 3, :], g * CPG + j, j % 3, g * 3 + j // 3)

                chunks(range(3))
                if not later(g, 1):
                    clear_slots(0, JOBS * 2 // 3)
                chunks(range(3, CPG))
                for t in range(G):
                    sp.wait_ge(kp_rdy, g * G + (t + 1))
                    for s, part in enumerate(K_PARTS):
                        sp.dma_start(kst[g * G + t, s * HD:(s + 1) * HD].rearrange("d h m -> h d m"),
                                     kparts[:, part, :]).then_inc(kp_out, 16)
                if earlier(g, NG - 1):
                    sp.wait_ge(o_ps, g * G + G)
                    context(g + 1)
                if not later(g, 1):
                    clear_slots(JOBS * 2 // 3, JOBS)

            steps(sp, NG, 1, 1, 1, lambda n, u, r: group(n))

        def attn1_gpsimd(pool):
            pool.memset(ident[:], 0.0).then_inc(consts, 1)
            pool.memset(ident16[:], 0.0).then_inc(consts, 1)
            pool.wait_ge(consts, 2)
            for m in (ident, ident16):
                pool.affine_select(out=m[:], in_=m[:], compare_op=ALU.not_equal, fill=1.0, base=0,
                                   pattern=[[-1, P]], channel_multiplier=1).then_inc(consts, 1)
            pool.memset(zeros, 0.0).then_inc(zero_set, 1)
            pool.memset(wsc[:, 1, :], WS).then_inc(scales, 1)
            pool.memset(mhalf[:], -0.5).then_inc(mhalf_set, 1)
            pool.wait_ge(mhalf_set, 1)
            for g in range(NG):
                norm_factors(0, XS, False, g * G, (g + 1) * G)
            pool.wait_ge(rms_in, 16)
            pool.tensor_scalar(wsc[:, 0, :], wsc[:, 0, :], WS, 1.0, ALU.mult, ALU.mult).then_inc(scales, 2)
            pool.wait_ge(scales, 3)
            prepare_router(0)

            def group(g):
                for t in range(G):
                    pool.wait_ge(cx_in, g * 16 + 16)
                    if later(g * G + t if isinstance(g, int) else g, 1):
                        wait_apart(pool, kp_out, (g * G + t) * STACKED)
                    n = (g * G + t) * 4
                    pool.tensor_scalar(kparts[:, 0, :], cx1[:, t, :], 1.0, 1.0, ALU.mult, ALU.mult).then_inc(kp_step, 1)
                    wait_apart(pool, kp_step, n + 1)
                    pool.tensor_tensor(krest, cx1[:, t, :], kparts[:, 0, :], ALU.subtract).then_inc(kp_step, 1)
                    wait_apart(pool, kp_step, n + 2)
                    pool.tensor_scalar(kparts[:, 1, :], krest, 1.0, 1.0, ALU.mult, ALU.mult).then_inc(kp_step, 1)
                    wait_apart(pool, kp_step, n + 3)
                    pool.tensor_tensor(kparts[:, 2, :], krest, kparts[:, 1, :], ALU.subtract).then_inc(kp_step, 1)
                    pool.wait_ge(kp_step, n + 4)
                    pool.nop().then_inc(kp_rdy, 1)

            steps(pool, NG, 1, 1, 1, lambda n, u, r: group(n))

        def attn1_scalar(act):
            def weights(j):
                act.wait_ge(w_in[j], 16)
                act.activation(w3[:, j, HI, :, :], wstage[j], ACT.Copy, scale=WS).then_inc(w_hi, 1)

            def columns(g):
                act.wait_ge(factors[0], g * FACTOR_STEPS + FACTOR_STEPS)
                for t in range(G):
                    if later(g * G + t if isinstance(g, int) else g, 1):
                        act.wait_ge(row_rdy, g * G + t)
                    n = g * G + t
                    act.activation(xn1, x[:, n, :], ACT.Identity, scale=rstd[:, bass.ds(n, 1)],
                                   bias=shift[:, bass.ds(n, 1)]).then_inc(xn_rdy, 1)
                for t in range(G):
                    act.wait_ge(t_ps, g * G + (t + 1))
                    act.activation(xt1[:, :, :, t, :], ps[:, t, :].bitcast(F16).rearrange("p (h e s) -> p h e s", h=2, e=DT),
                                   ACT.Copy).then_inc(xt_rdy, 1)

            def group(g):
                for t in range(G):
                    act.wait_ge(q_ps, g * G + (t + 1))
                    act.activation(qt[:, t, :, :], ps[:, 4 + t, :].rearrange("p (t s) -> p t s", t=G), ACT.Copy,
                                   scale=UNSCALE * SCORE).then_inc(q_rdy, 1)
                act.wait_ge(w_lo, 3)
                act.wait_ge(scales, 3)
                if later(g, 1):
                    act.wait_ge(zero_out, 16 * JOBS)
                for j in range(CPG):
                    c = g * CPG + j
                    act.wait_ge(chunk_in[0][j % 3], g * 48 + 16 * (j // 3 + 1))
                    act.activation(wgu[:, c, HI, :], stage[:, j % 3, :], ACT.Copy, scale=wsc[:, 0, bass.ds(c, 1)]).then_inc(gu_hi, 1)
                for t in range(G):
                    act.wait_ge(max_rdy, g * G + (t + 1))
                    act.activation(prob1[:, t, :], ps[:, t, 0:2 * P], ACT.Exp, bias=negmax1[:, t:t + 1],
                                   accum_out=rowsum1[:, t:t + 1]).then_inc(prob_rdy, 1)
                for t in range(G):
                    act.wait_ge(pt_ps, g * G + (t + 1))
                    act.activation(probt1[:, t, :, :], ps[:, 4 + t, 0:2 * P].rearrange("p (k q) -> p k q", k=2),
                                   ACT.Copy).then_inc(pt_rdy, 1)
                if earlier(g, NG - 1):
                    columns(g + 1)

            weights(0)
            columns(0)
            weights(1)
            weights(2)
            steps(act, NG, 1, 1, 1, lambda n, u, r: group(n))

        def attn1_vector(dve):
            def group_stats(g):
                dve.wait_ge(x_in[g], 16)
                for t in range(G):
                    tile_stats(dve, g * G + t, g * G + t, t % 2, 0)

            def weights(j):
                dve.wait_ge(w_hi, j + 1)
                dve.scalar_tensor_tensor(out=w3[:, j, LO, :, :], in0=wstage[j], scalar=WS, in1=w3[:, j, HI, :, :],
                                         op0=ALU.mult, op1=ALU.subtract).then_inc(w_lo, 1)

            def rows(g, t):
                dve.wait_ge(xn_rdy, g * G + (t + 1))
                dve.tensor_copy(rows1[:, t, HI, :], xn1).then_inc(hi_rdy, 1)
                dve.wait_ge(hi_rdy, g * G + (t + 1))
                dve.tensor_tensor(rows1[:, t, LO, :], xn1, rows1[:, t, HI, :], ALU.subtract).then_inc(row_rdy, 1)

            def group(g):
                def low_part(j):
                    c = g * CPG + j
                    dve.wait_ge(gu_hi, c + 1)
                    dve.scalar_tensor_tensor(out=wgu[:, c, LO, :], in0=stage[:, j % 3, :], scalar=wsc[:, 0, bass.ds(c, 1)],
                                             in1=wgu[:, c, HI, :], op0=ALU.mult, op1=ALU.subtract).then_inc(gu_lo, 1)

                for t in range(G):
                    dve.wait_ge(k_ps, g * G + (t + 1))
                    dve.tensor_scalar(kt[:, t, :, :], ps[:, t, :].rearrange("p (t s) -> p t s", t=G), UNSCALE, None,
                                      ALU.mult).then_inc(k_rdy, 1)
                    low_part(t)
                for t in range(G):
                    dve.wait_ge(v_ps, g * G + (t + 1))
                    dve.tensor_scalar(v1[:, t, :], ps[:, 4 + t, :], UNSCALE, None, ALU.mult).then_inc(v_rdy, 1)
                    low_part(G + t)
                low_part(2 * G)
                for t in range(G):
                    dve.wait_ge(s_ps, g * G + (t + 1))
                    if later(g, 1):
                        dve.wait_ge(x1_done, (g - 1) * G + (t + 1))
                    dve.tensor_reduce(negmax1[:, t:t + 1], ps[:, t, 0:2 * P], AX.X, ALU.max,
                                      negate=True).then_inc(max_rdy, 1)
                for t in range(G):
                    dve.wait_ge(prob_rdy, g * G + (t + 1))
                    dve.reciprocal(rinv1[:, t:t + 1], rowsum1[:, t:t + 1]).then_inc(rinv_rdy, 1)
                for t in range(G):
                    dve.wait_ge(o_ps, g * G + (t + 1))
                    dve.tensor_copy(ot1[:, t, :, :], ps[:, t, :].rearrange("p (e q) -> p e q", e=DT)).then_inc(o_rdy, 1)
                    if earlier(g, NG - 1):
                        rows(g + 1, t)
                dve.wait_ge(rinv_rdy, g * G + G)
                for t in range(G):
                    n = g * G + t
                    dve.wait_ge(y_ps, g * G + (t + 1))
                    dve.scalar_tensor_tensor(out=x[:, n, :], in0=ps[:, 4 + t, :], scalar=rinv1[:, t:t + 1],
                                             in1=x[:, n, :], op0=ALU.mult, op1=ALU.add).then_inc(x1_done, 1)
                    tile_stats(dve, n, g * G + (t + NT), t % 2, 1, x1_done, g * G + (t + 1))

            group_stats(0)
            weights(0)
            for t in range(G):
                rows(0, t)
            for j in range(1, 3):
                weights(j)
                group_stats(j)
            group_stats(3)
            steps(dve, NG, 1, 1, 1, lambda n, u, r: group(n))

        def attn1_tensor(pe):
            pe.wait_ge(consts, 4)

            def parts(outp, w, xx):
                last = None
                pairs = [(HI, HI), (HI, LO), (LO, HI)]
                for i, (p, q) in enumerate(pairs):
                    for t in range(DT):
                        last = pe.matmul(outp, w(p, t), xx(q, t), start=(i == 0 and t == 0),
                                         stop=(i == 2 and t == DT - 1))
                return last

            def columns(g, t):
                pe.wait_ge(row_rdy, g * G + (t + 1))
                tb = ps[:, t, :].bitcast(F16)
                for h in range(2):
                    for e in range(DT):
                        c = (h * DT + e) * P
                        last = pe.transpose(tb[:, c:c + P], rows1[:, t, h, e * P:(e + 1) * P], ident16[:])
                last.then_inc(t_ps, 1)

            for t in range(G):
                columns(0, t)

            def group(g):
                if not later(g, 1):
                    pe.wait_ge(w_lo, 1)
                pe.wait_ge(xt_rdy, g * G + G)
                for e in range(G):
                    if later(g, 1):
                        pe.wait_ge(x1_done, (g - 1) * G + (e + 1))
                    parts(ps[:, 4 + e, :], lambda p, t: w3[:, 0, p, t, e * P:(e + 1) * P],
                          lambda q, t: xt1[:, q, t, :, :]).then_inc(q_ps, 1)
                if not later(g, 1):
                    pe.wait_ge(w_lo, 2)
                for e in range(G):
                    parts(ps[:, e, :], lambda p, t: w3[:, 1, p, t, e * P:(e + 1) * P],
                          lambda q, t: xt1[:, q, t, :, :]).then_inc(k_ps, 1)
                if not later(g, 1):
                    pe.wait_ge(w_lo, 3)
                for t in range(G):
                    pe.wait_ge(q_rdy, g * G + (t + 1))
                    parts(ps[:, 4 + t, :], lambda p, e: xt1[:, p, e, t, :],
                          lambda q, e: w3[:, 2, q, e, :]).then_inc(v_ps, 1)
                pe.wait_ge(k_rdy, g * G + G)
                pe.wait_ge(ct_in, g * (16 * G) + 16 * G)
                for t in range(G):
                    for k, keys in enumerate((ct1[:, t, :, :], kt[:, :, t, :])):
                        for e in range(DT):
                            last = pe.matmul(ps[:, t, k * P:(k + 1) * P], qt[:, e, t, :], keys[:, e, :],
                                             start=(e == 0), stop=(e == DT - 1))
                    last.then_inc(s_ps, 1)
                for t in range(G):
                    pe.wait_ge(prob_rdy, g * G + (t + 1))
                    pe.wait_ge(v_rdy, g * G + (t + 1))
                    for k in range(2):
                        last = pe.transpose(ps[:, 4 + t, k * P:(k + 1) * P], prob1[:, t, k * P:(k + 1) * P], ident[:])
                    last.then_inc(pt_ps, 1)
                pe.wait_ge(cx_in, g * 16 + 16)
                for t in range(G):
                    pe.wait_ge(pt_rdy, g * G + (t + 1))
                    for e in range(DT):
                        for k, vals in enumerate((cx1[:, t, :], v1[:, t, :])):
                            last = pe.matmul(ps[:, t, e * P:(e + 1) * P], vals[:, e * P:(e + 1) * P],
                                             probt1[:, t, k, :], start=(k == 0), stop=(k == 1))
                    last.then_inc(o_ps, 1)
                if not later(g, 1):
                    pe.wait_ge(wo_in, 16)
                for t in range(G):
                    pe.wait_ge(o_rdy, g * G + (t + 1))
                    for e in range(DT):
                        last = pe.matmul(ps[:, 4 + t, :], ot1[:, t, e, :], wo[:, e, :], start=(e == 0), stop=(e == DT - 1))
                    last.then_inc(y_ps, 1)
                    if earlier(g, NG - 1):
                        columns(g + 1, t)

            steps(pe, NG, 1, 1, 1, lambda n, u, r: group(n))

        per_layer = dict(xn=NT, row_hi=NT, row=NT, t_ps=NT, xt=NT, r_ps=NT, lg=NT, wd_in=16, wd_rest_in=64, const=8, ex_rdy=1,
                         counts=1, pre_ps=1, routed=1, icol=4 * NT, comb=2 * NT, scat_rdy=1)
        for u in range(4):
            per_layer |= {f"scat_in{u}": 8 * NT, f"scat_out{u}": 8 * NT, f"brow_in{u}": 4 * NT,
                          f"crow_in{u}": 16 * ((JOBS + 3 - u) // 4), f"gath_in{u}": 8 * NT}
        for u in range(2):
            per_layer |= {f"row_out{u}": 8 * NT, f"y_out{u}": 16 * ((JOBS + 1 - u) // 2)}
        for part, total in (("b", NT), ("c", JOBS)):
            per_layer |= {part + n: total for n in ("xt", "gu_ps", "t_ps", "silu", "hid", "ht_ps", "ht", "y_ps", "y")}
        msem = {n: sem("m_" + n) for n in per_layer}
        route_step = [sem(f"route_step{k}") for k in range(2)]
        odds_rdy = sem("odds_rdy")

        def wait(eng, k, name, value):
            eng.wait_ge(msem[name], k * per_layer[name] + value)

        def wait_alone(eng, k, name, value):
            wait_apart(eng, msem[name], k * per_layer[name] + value)

        hrow_t = hrow.rearrange("(n p) d -> n p d", p=P)
        xslot_t = xslot.rearrange("(n p) d -> n p d", p=P)
        yslot_t = yslot.rearrange("(n p) d -> n p d", p=P)
        out_t = out.rearrange("(n p) d -> n p d", p=P)
        out_sent, ones_set = sem("out_sent"), sem("ones_set")

        def rows_scalar(act, k):
            s = msem

            def step(n, u, r):
                if earlier(n, NT):
                    if later(n, 2):
                        wait(act, k, "row", n - 1)
                    act.activation(xn2[:, u, :], x[:, n, :], ACT.Identity, scale=rstd[:, bass.ds(n, 1)],
                                   bias=shift[:, bass.ds(n, 1)]).then_inc(s["xn"], 1)
                if later(n, 2):
                    wait(act, k, "t_ps", n - 1)
                    if later(n, 4):
                        wait(act, k, "r_ps", n - 3)
                    act.activation(xt2[:, u, :, :, :], ps[:, u, :].bitcast(F16).rearrange("p (h e s) -> p h e s", h=2, e=DT),
                                   ACT.Copy).then_inc(s["xt"], 1)

            steps(act, NT + 2, 4, 2, 2, step)

        def rows_vector(dve, k):
            s = msem

            def step(n, u, r):
                if earlier(n, NT):
                    wait(dve, k, "xn", n + 1)
                    if later(n, 2):
                        wait(dve, k, "t_ps", n - 1)
                        wait(dve, k, f"row_out{u}", r * 16)
                    dve.tensor_copy(rowout[:, u, HI, :], xn2[:, u, :]).then_inc(s["row_hi"], 1)
                    wait(dve, k, "row_hi", n + 1)
                    dve.tensor_tensor(rowout[:, u, LO, :], xn2[:, u, :], rowout[:, u, HI, :],
                                      ALU.subtract).then_inc(s["row"], 1)
                if later(n, 3):
                    wait(dve, k, "r_ps", n - 2)
                    dve.tensor_scalar(lg[:, :, bass.ds(n - 3, 1)], ps[:, 3 - u, 0:E].unsqueeze(2), UNSCALE, None,
                                      ALU.mult).then_inc(s["lg"], 1)

            steps(dve, NT + 3, 4, 3, 2, step)

        def rows_tensor(pe, k):
            s = msem
            pe.wait_ge(rw_step[k], DT + 2)

            def step(n, u, r):
                if earlier(n, NT):
                    wait(pe, k, "row", n + 1)
                    if later(n, 2):
                        wait(pe, k, "xt", n - 1)
                    transposes(pe, ps[:, u, :], lambda h, e: rowout[:, u, h, e * P:(e + 1) * P]).then_inc(s["t_ps"], 1)
                if later(n, 1):
                    v = 1 - u
                    wait(pe, k, "xt", n)
                    if later(n, 3):
                        wait(pe, k, "lg", n - 2)
                    three(pe, ps[:, 2 + v, 0:E], lambda p, t: xt2[:, v, p, t, :],
                          lambda q, t: rwp[:, t, q, :], DT).then_inc(s["r_ps"], 1)

            steps(pe, NT + 1, 4, 1, 2, step)

        def rows_sync(sp, k):
            s = msem

            def step(n, u, r):
                wait(sp, k, "row", n + 1)
                sp.dma_start(hrow_t[n], rowout[:, u, :, :].rearrange("p h d -> p (h d)")).then_inc(s[f"row_out{u}"], 16)

            steps(sp, NT, 2, 2, 2, step)

        def transposes(pe, bank, rows):
            tb = bank.bitcast(F16)
            for h in range(2):
                for e in range(DT):
                    c = (h * DT + e) * P
                    last = pe.transpose(tb[:, c:c + P], rows(h, e), ident16[:])
            return last

        def three(pe, outp, w, xx, tiles):
            for i, (p, q) in enumerate([(HI, HI), (HI, LO), (LO, HI)]):
                for t in range(tiles):
                    last = pe.matmul(outp, w(p, t), xx(q, t), start=(i == 0 and t == 0),
                                     stop=(i == 2 and t == tiles - 1))
            return last

        def routing(dve, k):
            s = msem
            count = 0

            def then(ins):
                nonlocal count
                count += 1
                ins.then_inc(route_step[k], 1)
                dve.wait_ge(route_step[k], count)

            def by_tile(v):
                return v.rearrange("p e n -> p n e")

            def over_experts(v):
                return v.unsqueeze(1).broadcast_to([P, E, NT])

            def over_tiles(v):
                return v.unsqueeze(2).broadcast_to([P, E, NT])

            wait(dve, k, "const", 8)
            wait(dve, k, "lg", NT)
            then(dve.memset(ones8, 1.0))
            if k == 1:
                wait(dve, k, "ex_rdy", 1)
                then(dve.tensor_scalar(lg, lg, 1.0, None, ALU.add))
                then(dve.reciprocal(lg, lg))
            for top, idx, m, cand in ((top1, idx1, m1, lg), (top2, idx2, m2, z)):
                if m is m2:
                    yield
                if m is m2:
                    then(dve.scalar_tensor_tensor(out=z.rearrange("p e n -> p (e n)"), in0=m1.rearrange("p e n -> p (e n)"),
                                                  scalar=-3e38, in1=lg.rearrange("p e n -> p (e n)"),
                                                  op0=ALU.mult, op1=ALU.add))
                then(dve.tensor_reduce(top, by_tile(cand), AX.X, ALU.max))
                then(dve.tensor_tensor(m, cand, over_experts(top), ALU.is_equal))
                then(dve.tensor_tensor(m, m, em8, ALU.mult))
                then(dve.tensor_reduce(idx, by_tile(m), AX.X, ALU.min))
                then(dve.tensor_tensor(m, em8, over_experts(idx), ALU.is_equal))
            yield
            then(dve.tensor_tensor(asg, m1, m2, ALU.add))
            flat = "p e n -> p (e n)"
            then(dve.tensor_tensor_scan(cum.rearrange(flat), scanmask.rearrange(flat), asg.rearrange(flat), 0.0,
                                        ALU.mult, ALU.add))
            dve.nop().then_inc(s["counts"], 1)
            yield
            wait(dve, k, "pre_ps", 1)
            then(dve.tensor_scalar(tiles_i, ps[:, 4, F + E:F + 2 * E], float(P - 1), None, ALU.add))
            then(dve.tensor_scalar(tiles_i, tiles_i, 7, None, ALU.arith_shift_right))
            then(dve.tensor_copy(tiles_f, tiles_i))
            then(dve.tensor_tensor_scan(tiles_c, ones8, tiles_f, 0.0, ALU.mult, ALU.add))
            then(dve.tensor_tensor(base, tiles_c, tiles_f, ALU.subtract))
            then(dve.scalar_tensor_tensor(out=startpos, in0=base, scalar=float(P), in1=ps[:, 4, F:F + E],
                                          op0=ALU.mult, op1=ALU.add))
            yield
            then(dve.tensor_tensor(z, cum, asg, ALU.subtract))
            then(dve.tensor_tensor(z, z, over_tiles(startpos), ALU.add))
            for m, pos, idx in ((m1, pos1, idx1), (m2, pos2, idx2)):
                then(dve.tensor_tensor(m, m, z, ALU.mult))
                then(dve.tensor_reduce(idx, by_tile(m), AX.X, ALU.add))
                then(dve.tensor_copy(pos, idx))
            yield
            then(dve.memset(jexp, 0.0))
            for e in range(1, E):
                then(dve.scalar_tensor_tensor(out=jexp, in0=jidx, scalar=base[:, e:e + 1], in1=jexp,
                                              op0=ALU.is_ge, op1=ALU.add))
            yield
            then(dve.tensor_copy(eid, jexp))
            if k == 0:
                then(dve.tensor_tensor(ex, top2, top1, ALU.subtract))
                dve.nop().then_inc(odds_rdy, 1)
                then(dve.memset(s12, UNSCALE))
            else:
                then(dve.memset(w1, 1.0))
                then(dve.memset(w2, 1.0))
                then(dve.tensor_scalar(s12[:, 0, :], top1, UNSCALE, None, ALU.mult))
                then(dve.tensor_scalar(s12[:, 1, :], top2, UNSCALE, None, ALU.mult))
            dve.nop().then_inc(s["routed"], 1)
            yield
            if k == 0:
                wait(dve, k, "ex_rdy", 1)
                then(dve.tensor_scalar(w1, ex, 1.0, None, ALU.add))
                then(dve.reciprocal(w1, w1))
                then(dve.tensor_tensor(w2, ex, w1, ALU.mult))

        def route_tables(pool, k):
            s = msem
            pool.iota(em8, pattern=[[1, E], [0, NT]], base=-E, channel_multiplier=0, allow_small_or_imprecise_dtypes=True).then_inc(s["const"], 1)
            pool.iota(jidx, pattern=[[1, JOBS]], base=0, channel_multiplier=0, allow_small_or_imprecise_dtypes=True).then_inc(s["const"], 1)
            pool.memset(scanmask, 1.0).then_inc(s["const"], 1)
            pool.memset(ones, 1.0).then_inc(s["const"], 1)
            pool.memset(unscale, UNSCALE).then_inc(s["const"], 1)
            pool.memset(tri, 1.0).then_inc(s["const"], 1)
            wait(pool, k, "const", 6)
            pool.memset(scanmask[:, :, 0:1], 0.0).then_inc(s["const"], 1)
            pool.affine_select(out=tri, in_=tri, compare_op=ALU.is_gt, fill=0.0, base=0,
                               pattern=[[1, P]], channel_multiplier=-1).then_inc(s["const"], 1)

        def route_tensor(pe, k):
            s = msem
            wait(pe, k, "counts", 1)
            counts = cum[:, :, NT - 1:NT].rearrange("p e n -> p (e n)")
            pe.matmul(ps[:, 4, F:F + E], tri, counts, start=True, stop=True)
            pe.matmul(ps[:, 4, F + E:F + 2 * E], ones, counts, start=True, stop=True).then_inc(s["pre_ps"], 1)

        def scatter_gpsimd(pool, k):
            s = msem
            wait(pool, k, "routed", 1)
            pool.wait_ge(zero_out, 16 * JOBS)

            def step(n, u, r):
                wait(pool, k, f"scat_in{u}", r * 32 + 32)
                if later(n, 4):
                    wait(pool, k, f"scat_out{u}", r * 32)
                one = bass.ds(n, 1)
                pool.tensor_copy(icol[:, u, :], pos[:, n, :]).then_inc(s["icol"], 1)
                pool.tensor_copy(rowa[:, u, 2 * D:2 * D + 2].bitcast(F32), s12[:, 0, one]).then_inc(s["icol"], 1)
                pool.tensor_copy(rowb[:, u, 2 * D:2 * D + 2].bitcast(F32), s12[:, 1, one]).then_inc(s["icol"], 1)
                wait_alone(pool, k, "icol", n * 3 + 3)
                for j, buf in enumerate((rowa, rowb)):
                    pool.indirect_dma_start(out=xslot, out_offset=bass.IndirectOffsetOnAxis(ap=icol[:, u, j:j + 1], axis=0),
                                            in_=buf[:, u, :].bitcast(I32), in_offset=None).then_inc(s[f"scat_out{u}"], 16)

            steps(pool, NT, 4, 4, 4, step)
            for u in range(4):
                wait(pool, k, f"scat_out{u}", 32 * (NT // 4))
            pool.nop().then_inc(s["scat_rdy"], 1)

        def jobs_sync(sp, k, part, total):
            s = msem
            src = hrow_t if part == "b" else xslot_t
            width = 2 * D if part == "b" else 2 * D + 2
            if part == "b":
                for u in range(2):
                    wait(sp, k, f"row_out{u}", 16 * (NT // 2))
            else:
                wait(sp, k, "scat_rdy", 1)

            def load(n, u, r):
                buf = rowin[:, u, 0:width]
                sp.dma_start(buf if part == "b" else buf.bitcast(I32), src[n]).then_inc(s[f"{part}row_in{u}"], 16)

            def scatter_loads(n):
                v = n % 4
                if n >= 4:
                    wait(sp, k, f"scat_out{v}", n // 4 * 32)
                sp.dma_start(rowa[:, v, 0:2 * D], hrow_t[n]).then_inc(s[f"scat_in{v}"], 16)
                sp.dma_start(rowb[:, v, 0:2 * D], hrow_t[n]).then_inc(s[f"scat_in{v}"], 16)

            for n in range(4):
                if part == "c":
                    wait(sp, k, "bhid", NT - 3 + n)
                load(n, n, 0)

            def step(n, u, r):
                if later(n, 1) and part == "c":
                    v = (u + 1) % 2
                    wait(sp, k, "cy", n)
                    sp.dma_start(yslot_t[n - 1], yb[:, v, :]).then_inc(s[f"y_out{v}"], 16)
                if earlier(n, total - 4):
                    wait(sp, k, part + "hid", n + 1)
                    load(n + 4, u, r)

            if part == "b":
                last_weights = a[f"L{k}_d"].rearrange("e (f p) n -> p e f n", p=P)
                for n in range(4):
                    scatter_loads(n)
                for n in range(NT - 4):
                    step(n, n % 4, n // 4)
                    if n < 4:
                        sp.dma_start(wd[:, 2 * n:2 * n + 2, :, :], last_weights[:, 2 * n:2 * n + 2]).then_inc(s["wd_rest_in"], 16)
                    for m in range(2 * n - 4, 2 * n - 2):
                        if 4 <= m < NT:
                            scatter_loads(m)
            else:
                steps(sp, total + 1, 4, 8, 4, step)

        def jobs_tensor(pe, k, part, total):
            s = msem
            if part == "b":
                wait(pe, k, "wd_in", 16)
                pe.wait_ge(*((gu_lo, CHUNKS), (chunk_step, AHEAD + 3 * CHUNKS))[k])
            else:
                wait(pe, k, "routed", 1)
                wait(pe, k, "wd_rest_in", 64)
            wait(pe, k, "lg" if part == "b" else "bhid", NT)

            def rows_in(n, v, q):
                wait(pe, k, f"{part}row_in{v}", q * 16 + 16)
                if later(n, 2):
                    wait(pe, k, part + "xt", n - 1)
                transposes(pe, ps[:, 2 + v % 2, :], lambda h, e: rowin[:, v, h * D + e * P:h * D + (e + 1) * P]).then_inc(s[part + "t_ps"], 1)

            rows_in(0, 0, 0)
            expert = {}

            def step(n, w, r):
                u, v = w % 2, 1 - w % 2
                if part == "c":
                    before = expert.get(w - 1)
                    if before is None and later(n, 1):
                        before = pe.value_load(eid[0:1, bass.ds(n - 1, 1)], min_val=0, max_val=E - 1)
                    if earlier(n, total):
                        e = pe.value_load(eid[0:1, bass.ds(n, 1)], min_val=0, max_val=E - 1)
                    expert.clear()
                    expert[w] = e if earlier(n, total) else None
                if earlier(n, total):
                    wait(pe, k, part + "xt", n + 1)
                    if later(n, 2):
                        wait(pe, k, part + "hid", n - 1)
                    if part == "b":
                        first = lambda q, t: wgu[:, E * DT + t, q, :]
                    else:
                        first = lambda q, t: wgu[:, e * DT + t, q, :]
                    three(pe, ps[:, u, :], lambda p, t: xt2[:, u, p, t, :], first, DT).then_inc(s[part + "gu_ps"], 1)
                if earlier(n, total - 1):
                    rows_in(n + 1, (w + 1) % 4, r + (w + 1) // 4)
                if later(n, 1):
                    wait(pe, k, part + "ht", n)
                    if later(n, 3):
                        wait(pe, k, part + "y", n - 2)
                    elif part == "c" and n == 1:
                        wait(pe, k, "by", NT)
                    if part == "b":
                        second = lambda f: wd[:, E, f, :]
                    else:
                        second = lambda f: wd[:, before, f, :]
                    for f in range(FT):
                        last = pe.matmul(ps[:, 6 + v, :], ht[:, v, f, :], second(f), start=(f == 0), stop=(f == FT - 1))
                    last.then_inc(s[part + "y_ps"], 1)
                if earlier(n, total):
                    wait(pe, k, part + "hid", n + 1)
                    if later(n, 2):
                        wait(pe, k, part + "ht", n - 1)
                    for f in range(FT):
                        last = pe.transpose(ps[:, 4 + u, f * P:(f + 1) * P], hid[:, u, f * P:(f + 1) * P], ident[:])
                    last.then_inc(s[part + "ht_ps"], 1)

            def step_and_counts(n, w, r):
                step(n, w, r)
                if part == "b" and isinstance(n, int) and n == 1:
                    route_tensor(pe, k)

            steps(pe, total + 1, 4, 4 + (total + 1) % 4, 4, step_and_counts)

        def jobs_scalar(act, k, part, total):
            s = msem

            def columns_in(n, v):
                wait(act, k, part + "t_ps", n + 1)
                if later(n, 2):
                    wait(act, k, part + "gu_ps", n - 1)
                act.activation(xt2[:, v, :, :, :], ps[:, 2 + v, :].bitcast(F16).rearrange("p (h e s) -> p h e s", h=2, e=DT),
                               ACT.Copy).then_inc(s[part + "xt"], 1)

            columns_in(0, 0)

            def step(n, w, r):
                u = w % 2
                wait(act, k, part + "gu_ps", n + 1)
                if later(n, 2):
                    wait(act, k, part + "hid", n - 1)
                scale = unscale if part == "b" else rowin[:, w, 2 * D:2 * D + 2].bitcast(F32)
                act.activation(sg[:, u, :], ps[:, u, 0:F], ACT.Silu, scale=scale).then_inc(s[part + "silu"], 1)
                if earlier(n, total - 1):
                    columns_in(n + 1, 1 - u)
                wait(act, k, part + "ht_ps", n + 1)
                if later(n, 2):
                    wait(act, k, part + "y_ps", n - 1)
                act.activation(ht[:, u, :, :], ps[:, 4 + u, 0:F].rearrange("p (f s) -> p f s", f=FT),
                               ACT.Copy).then_inc(s[part + "ht"], 1)

            steps(act, total, 4, 4 if total % 4 == 0 else total % 4, 4, step)

        def jobs_vector(dve, k, part, total):
            s = msem
            stages = routing(dve, k) if part == "b" else iter(())

            def step(n, w, r):
                u, v = w % 2, 1 - w % 2
                if earlier(n, total):
                    wait(dve, k, part + "silu", n + 1)
                    if later(n, 2):
                        wait(dve, k, part + "ht_ps", n - 1)
                    scale = unscale if part == "b" else rowin[:, w, 2 * D:2 * D + 2].bitcast(F32)
                    dve.scalar_tensor_tensor(out=hid[:, u, :], in0=ps[:, u, F:2 * F], scalar=scale, in1=sg[:, u, :],
                                             op0=ALU.mult, op1=ALU.mult).then_inc(s[part + "hid"], 1)
                if isinstance(n, int) and n < 4:
                    next(stages, None)
                if later(n, 1):
                    wait(dve, k, part + "y_ps", n)
                    if part == "b":
                        dve.tensor_tensor(x[:, n - 1, :], x[:, n - 1, :], ps[:, 6 + v, :], ALU.add).then_inc(s["by"], 1)
                    else:
                        if later(n, 3):
                            wait(dve, k, f"y_out{v}", (r * 2 + (w - 1) // 2) * 16)
                        dve.tensor_copy(yb[:, v, :], ps[:, 6 + v, :]).then_inc(s["cy"], 1)
                if isinstance(n, int) and n < 3:
                    next(stages, None)

            steps(dve, total + 1, 4, 4 + (total + 1) % 4, 4, step)
            for _ in stages:
                pass

        def combine_gpsimd(pool, k):
            s = msem
            wait(pool, k, "y_out0", 16 * ((JOBS + 1) // 2))
            wait(pool, k, "y_out1", 16 * (JOBS // 2))

            def step(n, u, r):
                if later(n, 4):
                    wait(pool, k, "comb", n * 2 - 6)
                pool.tensor_copy(icol[:, u, :], pos[:, n, :]).then_inc(s["icol"], 1)
                wait_alone(pool, k, "icol", n + (3 * NT + 1))
                for j in range(2):
                    pool.indirect_dma_start(out=gy[:, u, j, :], out_offset=None, in_=yslot,
                                            in_offset=bass.IndirectOffsetOnAxis(ap=icol[:, u, j:j + 1], axis=0)
                                            ).then_inc(s[f"gath_in{u}"], 16)

            def step_and_factors(n, u, r):
                if k == 0 and isinstance(n, int) and n == NT - 4:
                    norm_factors(2, 1.0, False, 0, NT // 2)
                step(n, u, r)

            steps(pool, NT, 4, 4, 4, step_and_factors)

        def combine_vector(dve, k):
            s = msem
            if k == 0:
                dve.memset(ks[KR:KM, :, :, :], 1.0).then_inc(ones_set, 1)

            def step(n, u, r):
                stats_before = [lambda: None] * 3
                if k == 0 and later(n, 1):
                    stats_before = stat_steps(dve, n - 1, n + (2 * NT - 1), (u + 1) % 2, 2, s["comb"], n * 2)
                for j, w in enumerate((w1, w2)):
                    if earlier(n, NT):
                        if j == 0:
                            wait(dve, k, f"gath_in{u}", r * 32 + 32)
                        else:
                            wait(dve, k, "comb", n * 2 + 1)
                        dve.scalar_tensor_tensor(out=x[:, n, :], in0=gy[:, u, j, :], scalar=w[:, bass.ds(n, 1)],
                                                 in1=x[:, n, :], op0=ALU.mult, op1=ALU.add).then_inc(s["comb"], 1)
                    stats_before[j]()
                stats_before[2]()

            steps(dve, NT + 1, 4, 5, 4, step)

        def combine_sync(sp, k):
            def step(n, u, r):
                wait(sp, k, "comb", n * 2 + 2)
                sp.dma_start(out_t[n], x[:, n, :]).then_inc(out_sent, 16)

            steps(sp, NT, 2, 2, 2, step)
            sp.wait_ge(out_sent, 16 * NT)

        def moe_sync(sp, k):
            s = msem
            sp.wait_ge(stats_rdy[2 * k + 1], NT)
            last_weights = a[f"L{k}_d"].rearrange("e (f p) n -> p e f n", p=P)
            sp.dma_start(wd[:, E, :, :], last_weights[:, E]).then_inc(s["wd_in"], 16)
            rows_sync(sp, k)
            jobs_sync(sp, k, "b", NT)
            jobs_sync(sp, k, "c", JOBS)
            if k == 1:
                combine_sync(sp, k)

        def moe_gpsimd(pool, k):
            if k == 0:
                norm_factors(1, XS, True, 0, NT - G)
            norm_factors(2 * k + 1, XS, k == 0, NT - G, NT)
            route_tables(pool, k)
            scatter_gpsimd(pool, k)
            combine_gpsimd(pool, k)

        def moe_scalar(act, k):
            s = msem
            act.wait_ge(factors[2 * k + 1], 2 * FACTOR_STEPS)
            rows_scalar(act, k)
            if k == 1:
                wait(act, k, "lg", NT)
                act.activation(lg, lg, ACT.Exp, scale=-1.0).then_inc(s["ex_rdy"], 1)
            wait(act, k, "const", 8)
            jobs_scalar(act, k, "b", NT)
            if k == 0:
                act.wait_ge(odds_rdy, 1)
                act.activation(ex, ex, ACT.Exp).then_inc(s["ex_rdy"], 1)
            jobs_scalar(act, k, "c", JOBS)

        def moe_vector(dve, k):
            rows_vector(dve, k)
            jobs_vector(dve, k, "b", NT)
            jobs_vector(dve, k, "c", JOBS)
            combine_vector(dve, k)

        def moe_tensor(pe, k):
            rows_tensor(pe, k)
            wait(pe, k, "const", 8)
            jobs_tensor(pe, k, "b", NT)
            jobs_tensor(pe, k, "c", JOBS)

        stack_in = [sem(f"stack_in{u}") for u in range(4)]
        qn_rdy, qp_step, qp_rdy, qst_out = sem("qn_rdy"), sem("qp_step"), sem("qp_rdy"), sem("qst_out")
        s3_ps, max3_rdy, mt_ps, nm_step, nm_rdy, maxrow_in = [sem(n) for n in (
            "s3_ps", "max3_rdy", "mt_ps", "nm_step", "nm_rdy", "maxrow_in")]
        st_ps, exp_rdy, pv_ps, osb_rdy, rden_rdy, att_step, x3_done = [sem(n) for n in (
            "st_ps", "exp_rdy", "pv_ps", "osb_rdy", "rden_rdy", "att_step", "x3_done")]
        align_in = [sem(f"align_in{w}") for w in range(2)]
        rsum_out, rsum_in = sem("rsum_out"), [sem(f"rsum_in{v}") for v in range(2)]
        ct3_in, va_rdy = sem("ct3_in"), sem("va_rdy")
        ALIGN = 16 * 5

        def attn2_sync(sp):
            wait(sp, 0, "cy", JOBS)
            sp.wait_ge(kp_out, STACKED * NT)
            ctT = a["ctxT"].rearrange("b (e p) s -> b p e s", p=P)

            def parts_out(b, v):
                wait_apart(sp, qp_rdy, b + 1)
                for s, part in enumerate(Q_PARTS):
                    sp.dma_start(qst[v, s * HD:(s + 1) * HD].rearrange("d h m -> h d m"), qparts[:, part, :]).then_inc(qst_out, 16)

            def load(b, half, slot, v):
                sp.wait_ge(qst_out, b * STACKED + STACKED)
                sp.dma_start(ks[0:KR, slot, :, :], kst[b, :, 4 * half:4 * half + 4, :]).then_inc(stack_in[slot], 16)
                sp.dma_start(qs[0:KR, slot, :, :], qst[v, :, 4 * half:4 * half + 4, :]).then_inc(stack_in[slot], 16)

            def columns(b, v):
                sp.dma_start(ct3[:, v, :, :], ctT[b]).then_inc(ct3_in, 16)

            def max_rows(q, u):
                sp.wait_ge(nm_rdy, q + 1)
                for j in range(MAX_PARTS):
                    sp.dma_start(qs[KR + j:KR + j + 1, u, :, :], nm[0:16, j, :]).then_inc(maxrow_in, 16)

            sp.dma_start(rw[:], a["L1_rw"]).then_inc(rw_in[1], 16)
            parts_out(0, 0)
            load(0, 0, 0, 0)
            load(0, 1, 1, 0)
            parts_out(1, 1)
            sp.wait_ge(stats_rdy[2], NT)
            columns(0, 0)
            load(1, 0, 2, 1)
            max_rows(0, 0)

            def step(q, u, r):
                b, v = r * 2 + u // 2, u // 2
                if u % 2 == 0 and later(q, 4) and earlier(q, QUADS + 3):
                    wait_apart(sp, rden_rdy, b - 1)
                    sp.dma_start(rsum[v].rearrange("h (r m) -> (h r) m", r=HD), sums[:, v, :]).then_inc(rsum_out, 16)
                if u % 2 == 0 and earlier(q, QUADS - 2):
                    sp.wait_ge(va_rdy, b + 1)
                    columns(b + 1, 1 - v)
                if earlier(q, QUADS - 3):
                    if later(q, 1):
                        sp.wait_ge(st_ps, q * 16)
                    load(r * 2 + (u + 3) // 2, (u + 1) % 2, (u + 3) % 4, ((u + 3) // 2) % 2)
                if u % 2 == 0 and later(q, 4) and earlier(q, QUADS + 3):
                    wait_apart(sp, rsum_out, b * 16 - 16)
                    sp.dma_start(den[:, v, :], rsum[v].unsqueeze(1).broadcast_to([H, HD, D])).then_inc(rsum_in[v], 16)
                if earlier(q, QUADS - 1):
                    max_rows(q + 1, (u + 1) % 4)
                if later(q, 1) and earlier(q, QUADS + 1):
                    wait_apart(sp, osb_rdy, q)
                    w, row, bv = (u + 1) % 2, 64 * ((u + 1) % 2), ((u + 3) % 4) // 2
                    if w == 0 and later(q, 5):
                        sp.wait_ge(x3_done, b - 1)
                    for h in range(4):
                        sp.dma_start(num[row + h * HD:row + (h + 1) * HD, bv, :], osb[32 * h:32 * h + HD, w, :]).then_inc(align_in[w], 16)
                    sp.dma_start(sums[row:row + 4 * HD, bv, :], osb[HD:P:2 * HD, w, :]).then_inc(align_in[w], 16)
                if u % 2 == 0 and earlier(q, QUADS - 4):
                    loaded = r * 32 + 32 if isinstance(r, int) else sp.snap(r * 32 + 32)
                    wait_apart(sp, stack_in[2 * v], loaded)
                    wait_apart(sp, stack_in[2 * v + 1], loaded)
                    parts_out(b + 2, v)
                if u % 2 == 0 and later(q, 4) and earlier(q, QUADS - 4):
                    for j in range(3):
                        load_chunk(sp, 1, stage3[:, j, :], b * 3 + (j - 6), j, b - 2)

            steps(sp, QUADS + 4, 4, 8, 4, step)

        def attn2_gpsimd(pool):
            def prepare_chunk(buf, c, r, u):
                wait_apart(pool, chunk_in[1][u], 16 * (r + 1))
                scale = wsc[:, 1, bass.ds(c, 1)].broadcast_to([P, 2 * F])
                pool.tensor_tensor(wgu[:, c, HI, :], buf, scale, ALU.mult).then_inc(chunk_step, 1)
                wait_apart(pool, chunk_step, c * 3 + (AHEAD + 1))
                pool.tensor_tensor(buf, buf, scale, ALU.mult).then_inc(chunk_step, 1)
                wait_apart(pool, chunk_step, c * 3 + (AHEAD + 2))
                pool.tensor_tensor(wgu[:, c, LO, :], buf, wgu[:, c, HI, :], ALU.subtract).then_inc(chunk_step, 1)


            def parts(b):
                pool.wait_ge(qn_rdy, b + 1)
                if later(b, 1):
                    wait_apart(pool, qst_out, b * STACKED)
                n = b * 4
                pool.tensor_scalar(qparts[:, 0, :], qn, 1.0, 1.0, ALU.mult, ALU.mult).then_inc(qp_step, 1)
                wait_apart(pool, qp_step, n + 1)
                pool.tensor_tensor(qn, qn, qparts[:, 0, :], ALU.subtract).then_inc(qp_step, 1)
                wait_apart(pool, qp_step, n + 2)
                pool.tensor_scalar(qparts[:, 1, :], qn, 1.0, 1.0, ALU.mult, ALU.mult).then_inc(qp_step, 1)
                wait_apart(pool, qp_step, n + 3)
                pool.tensor_tensor(qparts[:, 2, :], qn, qparts[:, 1, :], ALU.subtract).then_inc(qp_step, 1)
                pool.wait_ge(qp_step, n + 4)
                pool.nop().then_inc(qp_rdy, 1)

            def values(b, v):
                wait_apart(pool, ct3_in, b * 16 + 16)
                if later(b, 2):
                    wait_apart(pool, pv_ps, b * 8 - 8)
                pool.tensor_copy(va[:, v, :, :, 0:HD], ct3[:, v, :, :].rearrange("p e (h d) -> p e h d", h=H)).then_inc(va_rdy, 1)

            pool.nop().then_inc(chunk_step, AHEAD)
            parts(0)
            norm_factors(2, 1.0, False, NT // 2, NT)
            parts(1)
            values(0, 0)

            def step(q, u, r):
                b, v = r * 2 + u // 2, u // 2
                if u % 2 == 0:
                    if earlier(q, QUADS - 4):
                        parts(b + 2)
                    if earlier(q, QUADS - 2):
                        values(b + 1, 1 - v)
                    if later(q, 4):
                        wait_apart(pool, rsum_in[v], r * 16)
                        pool.tensor_tensor(num[:, v, :], num[:, v, :], den[:, v, :], ALU.mult).then_inc(att_step, 1)
                        wait_apart(pool, att_step, b - 1)
                        pool.tensor_tensor(x[:, b - 2, :], x[:, b - 2, :], num[:, v, :], ALU.add).then_inc(x3_done, 1)
                elif later(q, 5) and earlier(q, QUADS - 4):
                    for j in range(3):
                        prepare_chunk(stage3[:, j, :], b * 3 + (j - 6), b - 2, j)

                if isinstance(q, int) and q == QUADS + 1:
                    prepare_router(1)
                    norm_factors(3, XS, False, 0, NT - G)

            steps(pool, QUADS + 4, 4, 8, 4, step)

        def attn2_scalar(act):
            act.wait_ge(factors[2], FACTOR_STEPS)

            def normed(b):
                if later(b, 1):
                    act.wait_ge(qp_step, b * 4)
                one = bass.ds(b, 1)
                act.activation(qn, x[:, b, :], ACT.Identity, scale=rstd[:, one], bias=shift[:, one]).then_inc(qn_rdy, 1)

            normed(0)
            normed(1)
            act.wait_ge(factors[2], 2 * FACTOR_STEPS)

            def results_out(q, w, moved):
                act.wait_ge(pv_ps, q * 4 + 4)
                if later(q, 2):
                    act.wait_ge(align_in[w], moved * ALIGN)
                act.activation(osb[:, w, :], ps[:, 6, :], ACT.Copy).then_inc(osb_rdy, 1)

            def step(q, u, r):
                for e in range(DT):
                    if later(q, 1) or e >= 2:
                        act.wait_ge(pv_ps, q * 4 + (e - 1))
                    for h in range(4):
                        n = 4 * e + h
                        act.wait_ge(st_ps, q * 16 + (n + 1))
                        act.activation(prob3[:, e % 2, h, :], ps[:, 4 + n % 2, :], ACT.Exp, scale=HEAD_SCORE).then_inc(exp_rdy, 1)
                    if e == 0 and later(q, 1):
                        results_out(q - 1, (u + 1) % 2, r * 2 + (u - 1) // 2)
                    if e == 2 and u % 2 == 0 and earlier(q, QUADS - 4):
                        normed(r * 2 + (u // 2 + 2))

            steps(act, QUADS, 4, 4, 4, step)
            results_out(QUADS - 1, 1, NT - 1)

        def attn2_vector(dve):
            def maxima(q, v, between):
                if later(q, 2):
                    dve.wait_ge(mt_ps, q - 1)
                for n in range(8):
                    dve.wait_ge(s3_ps, q * 8 + (n + 1))
                    dve.tensor_reduce(mx[:, v, 2 * n:2 * n + 2], ps[:, 2 * (n % 2):2 * (n % 2) + 2, :], AX.X, ALU.max,
                                      negate=True).then_inc(max3_rdy, 1)
                    between.get(n, lambda: None)()

            def max_parts(q):
                dve.wait_ge(mt_ps, q + 1)
                if later(q, 1):
                    dve.wait_ge(maxrow_in, q * (16 * MAX_PARTS))
                m = ps[0:16, 7, 0:P]
                dve.tensor_copy(nm[0:16, 0, :], m).then_inc(nm_step, 1)
                dve.wait_ge(nm_step, q + 1)
                dve.tensor_tensor(nm[0:16, 1, :], m, nm[0:16, 0, :], ALU.subtract).then_inc(nm_rdy, 1)

            dve.wait_ge(stats_rdy[2], NT)
            dve.memset(va[:, :, :, :, HD:2 * HD], 1.0).then_inc(ones_set, 1)
            maxima(0, 0, {})
            max_parts(0)
            maxima(1, 1, {})

            def step(q, u, r):
                b, v = r * 2 + u // 2, u // 2
                todo = {}
                if earlier(q, QUADS - 1):
                    todo[2] = lambda: max_parts(q + 1)
                if u % 2 == 1 and later(q, 3) and earlier(q, QUADS + 2):
                    def one_over_sums():
                        for w in range(2):
                            dve.wait_ge(align_in[w], b * ALIGN)
                        dve.reciprocal(sums[:, 1 - v, :], sums[:, 1 - v, :]).then_inc(rden_rdy, 1)
                    todo[7] = one_over_sums
                if u % 2 == 1 and later(q, 5):
                    todo[5] = lambda: tile_stats(dve, b - 2, b + (3 * NT - 2), v, 3, x3_done, b - 1)
                if earlier(q, QUADS - 2):
                    maxima(q + 2, u % 2, todo)
                else:
                    for n in sorted(todo):
                        todo[n]()

            steps(dve, QUADS + 4, 4, 8, 4, step)

        def attn2_tensor(pe):
            def maxima(q, slot, r, n):
                if n == 0:
                    pe.wait_ge(stack_in[slot], r * 32 + 32)
                if later(q, 1) or n >= 2:
                    pe.wait_ge(max3_rdy, q * 8 + (n - 1))
                for m in (2 * (n % 2), 2 * (n % 2) + 1):
                    last = pe.matmul(ps[:, m, :], qs[0:KR, slot, n // 2, m * P:(m + 1) * P], ks[0:KR, slot, n // 2, :],
                                     start=True, stop=True)
                last.then_inc(s3_ps, 1)

            def turn_maxima(q, v):
                pe.wait_ge(max3_rdy, q * 8 + 8)
                if later(q, 1):
                    pe.wait_ge(nm_rdy, q)
                pe.transpose(ps[0:16, 7, 0:P], mx[:, v, :], ident[:]).then_inc(mt_ps, 1)

            def products(q, e, half, v, b):
                pe.wait_ge(exp_rdy, q * 16 + (4 * e + 4))
                if e == 0:
                    pe.wait_ge(va_rdy, b + 1)
                    if later(q, 1):
                        pe.wait_ge(osb_rdy, q)
                for h in range(4):
                    last = pe.matmul(ps[2 * HD * h:2 * HD * (h + 1), 6, :], va[:, v, e, 4 * half + h, :],
                                     prob3[:, e % 2, h, :], start=(e == 0), stop=(e == DT - 1))
                last.then_inc(pv_ps, 1)

            for q in range(2):
                for n in range(8):
                    maxima(q, q, 0, n)
                if q == 0:
                    turn_maxima(0, 0)
            pe.wait_ge(ones_set, 2)

            def step(q, u, r):
                b = r * 2 + u // 2
                before = (u + 3) % 4
                pe.wait_ge(maxrow_in, q * (16 * MAX_PARTS) + 16 * MAX_PARTS)
                for e in range(DT):
                    def scores(h):
                        n = 4 * e + h
                        if later(q, 1) or n >= 2:
                            pe.wait_ge(exp_rdy, q * 16 + (n - 1))
                        pe.matmul(ps[:, 4 + n % 2, :], ks[0:KM, u, h, e * P:(e + 1) * P], qs[0:KM, u, h, :],
                                  start=True, stop=True).then_inc(st_ps, 1)

                    def next_maxima(half):
                        if earlier(q, QUADS - 2):
                            maxima(q + 2, (u + 2) % 4, r + (u + 2) // 4, 2 * e + half)

                    scores(0)
                    next_maxima(0)
                    scores(1)
                    if e >= 1:
                        products(q, e - 1, u % 2, u // 2, b)
                    elif later(q, 1):
                        products(q - 1, DT - 1, before % 2, before // 2, b)
                    scores(2)
                    scores(3)
                    if e == 1 and earlier(q, QUADS - 1):
                        turn_maxima(q + 1, (u + 1) % 2)
                    next_maxima(1)

            steps(pe, QUADS, 4, 4, 4, step)
            products(QUADS - 1, DT - 1, 1, 1, NT - 1)

        block = ctx.enter_context(nc.Block())

        @block.sync
        def _(sp):
            attn1_sync(sp)
            moe_sync(sp, 0)
            attn2_sync(sp)
            moe_sync(sp, 1)

        @block.gpsimd
        def _(pool):
            attn1_gpsimd(pool)
            moe_gpsimd(pool, 0)
            attn2_gpsimd(pool)
            moe_gpsimd(pool, 1)

        @block.scalar
        def _(act):
            attn1_scalar(act)
            moe_scalar(act, 0)
            attn2_scalar(act)
            moe_scalar(act, 1)

        @block.vector
        def _(dve):
            attn1_vector(dve)
            moe_vector(dve, 0)
            attn2_vector(dve)
            moe_vector(dve, 1)

        @block.tensor
        def _(pe):
            attn1_tensor(pe)
            moe_tensor(pe, 0)
            attn2_tensor(pe)
            moe_tensor(pe, 1)


def kernel(x, ctx_2048, mask_BxSx4224_bf0, L0_xattn_wq, L0_xattn_wk, L0_xattn_wv, L0_xattn_wo,
           L0_ffn_rms_weight, L0_ffn_router_w, L0_ffn_w_gate, L0_ffn_w_up, L0_ffn_w_down,
           L0_ffn_sw_gate, L0_ffn_sw_up, L0_ffn_sw_down, L1_ffn_gate_w, L1_ffn_w1, L1_ffn_w2, L1_ffn_w3,
           L1_ffn_ws1, L1_ffn_ws2, L1_ffn_ws3):
    import numpy as _np
    import concourse.bacc as _bacc
    from concourse import mybir as _mybir
    from concourse.bass_utils import run_bass_kernel_spmd as _run

    def first(gate, up, s_gate, s_up):
        w = _np.concatenate([_np.concatenate([gate, s_gate[None]]), _np.concatenate([up, s_up[None]])], axis=2)
        return w.reshape(CHUNKS, P, 2 * F)

    def flip(w):
        return _np.asarray(w).transpose(0, 2, 1)

    def n(v):
        return _np.asarray(v)

    arrays = {
        "x": n(x).reshape(T, D),
        "ctx": n(ctx_2048).reshape(T, D),
        "ctxT": n(ctx_2048).transpose(0, 2, 1),
        "wqT": n(L0_xattn_wq).T, "wkT": n(L0_xattn_wk).T, "wvT": n(L0_xattn_wv).T, "woT": n(L0_xattn_wo).T,
        "rms": _np.tile(n(L0_ffn_rms_weight).reshape(DT, P).T, (1, NE)),
        "L0_rw": n(L0_ffn_router_w).reshape(DT, P, E).transpose(1, 0, 2),
        "L1_rw": n(L1_ffn_gate_w).T.reshape(DT, P, E).transpose(1, 0, 2),
        "L0_gu": first(n(L0_ffn_w_gate), n(L0_ffn_w_up), n(L0_ffn_sw_gate), n(L0_ffn_sw_up)),
        "L0_d": _np.concatenate([n(L0_ffn_w_down), n(L0_ffn_sw_down)[None]]),
        "L1_gu": first(flip(L1_ffn_w1), flip(L1_ffn_w3), n(L1_ffn_ws1).T, n(L1_ffn_ws3).T),
        "L1_d": _np.concatenate([flip(L1_ffn_w2), n(L1_ffn_ws2).T[None]]),
    }
    arrays = {k: _np.ascontiguousarray(v) for k, v in arrays.items()}
    nc = _bacc.Bacc("TRN2", target_bir_lowering=False, num_devices=1)
    aps = {k: nc.dram_tensor("in_" + k, v.shape, _mybir.dt.from_np(v.dtype), kind="ExternalInput").ap()
           for k, v in arrays.items()}
    out = nc.dram_tensor("out_0", (T, D), _mybir.dt.float32, kind="ExternalOutput").ap()
    build(nc, aps, out)
    r = _run(nc, [{"in_" + k: v for k, v in arrays.items()}], core_ids=[0])
    return r.results[0]["out_0"].reshape(B, P, D)
```
